# Optimizing a Trainium2 kernel written in Bass

```python
import numpy as np
import jax
import jax.numpy as jnp

def _softmax(x, axis=-1):
    return jax.nn.softmax(x, axis=axis)

def _gelu(x):
    return jax.nn.gelu(x, approximate=True)

def _silu(x):
    return jax.nn.silu(x)

def _sigmoid(x):
    return jax.nn.sigmoid(x)

def _layernorm(x, axis=-1, eps=1e-05):
    m = jnp.mean(x, axis=axis, keepdims=True)
    v = jnp.var(x, axis=axis, keepdims=True)
    return (x - m) / jnp.sqrt(v + eps)

def _scatter_add(tgt, idx, src, axis=0):
    return tgt.at[idx].add(src)

def _segment_sum(src, seg, n):
    return jax.ops.segment_sum(src, seg, n)
kernel_name = 'mk_audio_tower_d1_tok_audfeat512_r4_428c8b'

def setup_inputs(seed: int=0):
    np.random.seed(seed)
    _w = jnp.asarray

    def _rec_inputs():
        import jax
        import jax.numpy as jnp
        _rk = jax.random.key(seed)
        x = 7.22013e-05 + 1.00017 * jax.random.normal(jax.random.fold_in(_rk, 1), (16, 512, 128), jnp.float32)
        return x
    x = _rec_inputs()

    def _L0_tok_setup():
        import jax, jax.numpy as jnp
        import numpy as np
        PATCH_SIZES = [8, 16, 32]
        STRIDE_RATIO = 0.5
        CTX = 512
        NUM_FEATURES = 128
        D_MODEL = 128
        BATCH = 32

        def _n_patches(p):
            s = max(1, int(p * STRIDE_RATIO))
            return (CTX - p) // s + 1

        def _extract_patches(x, patch_size, stride):
            n = (x.shape[1] - patch_size) // stride + 1
            idx = jnp.arange(n)[:, None] * stride + jnp.arange(patch_size)[None, :]
            w = x[:, idx, :]
            return w.reshape(x.shape[0], n, patch_size * x.shape[2])

        def _forward(x, W0, b0, pos0, W1, b1, pos1, W2, b2, pos2, scale_emb):
            params = [(W0, b0, pos0), (W1, b1, pos1), (W2, b2, pos2)]
            outs = []
            for i, (p, (W, b, pos)) in enumerate(zip(PATCH_SIZES, params)):
                s = max(1, int(p * STRIDE_RATIO))
                pt = _extract_patches(x, p, s)
                y = jnp.einsum('bnk,dk->bnd', pt, W) + b
                n = pt.shape[1]
                y = y + pos[:, :n, :] + scale_emb[i]
                outs.append(y)
            return jnp.concatenate(outs, axis=1)
        key = jax.random.key(seed)
        ks = jax.random.split(key, 12)
        inp = {'x': jax.random.normal(ks[0], (BATCH, CTX, NUM_FEATURES), dtype=jnp.float32)}
        for i, p in enumerate(PATCH_SIZES):
            k_in = p * NUM_FEATURES
            n = _n_patches(p)
            inp[f'W{i}'] = jax.random.normal(ks[1 + 3 * i], (D_MODEL, k_in), dtype=jnp.float32) / np.sqrt(k_in)
            inp[f'b{i}'] = jax.random.normal(ks[2 + 3 * i], (D_MODEL,), dtype=jnp.float32) / np.sqrt(k_in)
            inp[f'pos{i}'] = 0.02 * jax.random.normal(ks[3 + 3 * i], (1, n, D_MODEL), dtype=jnp.float32)
        inp['scale_emb'] = jax.random.normal(ks[10], (len(PATCH_SIZES), D_MODEL), dtype=jnp.float32)
        return inp
    _L0_tok_all = _L0_tok_setup()
    _L0_tok_in = {k: v for k, v in _L0_tok_all.items() if k in ('W0', 'b0', 'pos0', 'W1', 'b1', 'pos1', 'W2', 'b2', 'pos2', 'scale_emb')}
    del _L0_tok_all

    def _L0_attn_setup():
        import jax, jax.numpy as jnp
        import numpy as np
        from math import sqrt
        key = jax.random.key(seed)
        k1, k2, k3, k4 = jax.random.split(key, 4)
        bs, N, D, H = (2, 1024, 128, 8)
        z = jax.random.normal(k1, (bs, N, D), dtype=jnp.float32)
        w_qkv = jax.random.normal(k2, (3 * D, D), dtype=jnp.float32) * (1.0 / sqrt(D))
        w_agg = jax.random.normal(k3, (D, D), dtype=jnp.float32) * (1.0 / sqrt(D))
        b_agg = jax.random.normal(k4, (D,), dtype=jnp.float32) * 0.01
        return {'z': z, 'w_qkv': w_qkv, 'w_agg': w_agg, 'b_agg': b_agg}
    _L0_attn_all = _L0_attn_setup()
    _L0_attn_in = {k: v for k, v in _L0_attn_all.items() if k in ('w_qkv', 'w_agg', 'b_agg')}
    del _L0_attn_all

    def _L0_ffn_setup():
        import jax, jax.numpy as jnp
        import numpy as np
        NUM_EXPERTS = 8
        TOP_K = 2
        key = jax.random.key(seed)
        k0, k1, k2, k3, k4 = jax.random.split(key, 5)
        sl, bs, hs, ffn = (512, 2, 128, 512)
        T = sl * bs
        x = jax.random.normal(k0, (sl, bs, hs), jnp.float32)
        expert_weights = jax.random.uniform(k1, (T, TOP_K), jnp.float32)
        expert_indices = jax.random.randint(k2, (T, TOP_K), 0, NUM_EXPERTS)
        w1 = jax.random.normal(k3, (NUM_EXPERTS, hs, ffn), jnp.float32) * hs ** (-0.5)
        w2 = jax.random.normal(k4, (NUM_EXPERTS, ffn, hs), jnp.float32) * ffn ** (-0.5)
        return dict(x=x, expert_weights=expert_weights, expert_indices=expert_indices, w1=w1, w2=w2)
    _L0_ffn_all = _L0_ffn_setup()
    _L0_ffn_in = {k: v for k, v in _L0_ffn_all.items() if k in ('expert_weights', 'expert_indices', 'w1', 'w2')}
    del _L0_ffn_all
    return {'x': x, 'L0_tok_W0': _L0_tok_in['W0'], 'L0_tok_b0': _L0_tok_in['b0'], 'L0_tok_pos0': _L0_tok_in['pos0'], 'L0_tok_W1': _L0_tok_in['W1'], 'L0_tok_b1': _L0_tok_in['b1'], 'L0_tok_pos1': _L0_tok_in['pos1'], 'L0_tok_W2': _L0_tok_in['W2'], 'L0_tok_b2': _L0_tok_in['b2'], 'L0_tok_pos2': _L0_tok_in['pos2'], 'L0_tok_scale_emb': _L0_tok_in['scale_emb'], 'L0_attn_w_qkv': _L0_attn_in['w_qkv'], 'L0_attn_w_agg': _L0_attn_in['w_agg'], 'L0_attn_b_agg': _L0_attn_in['b_agg'], 'L0_ffn_expert_weights': _L0_ffn_in['expert_weights'], 'L0_ffn_expert_indices': _L0_ffn_in['expert_indices'], 'L0_ffn_w1': _L0_ffn_in['w1'], 'L0_ffn_w2': _L0_ffn_in['w2']}

def reference(x, L0_tok_W0, L0_tok_b0, L0_tok_pos0, L0_tok_W1, L0_tok_b1, L0_tok_pos1, L0_tok_W2, L0_tok_b2, L0_tok_pos2, L0_tok_scale_emb, L0_attn_w_qkv, L0_attn_w_agg, L0_attn_b_agg, L0_ffn_expert_weights, L0_ffn_expert_indices, L0_ffn_w1, L0_ffn_w2):
    import jax
    import jax.numpy as jnp

    def _L0_tok_ref(x, W0, b0, pos0, W1, b1, pos1, W2, b2, pos2, scale_emb):
        import jax, jax.numpy as jnp
        import numpy as np
        PATCH_SIZES = [8, 16, 32]
        STRIDE_RATIO = 0.5
        CTX = 512
        NUM_FEATURES = 128
        D_MODEL = 128
        BATCH = 32

        def _n_patches(p):
            s = max(1, int(p * STRIDE_RATIO))
            return (CTX - p) // s + 1

        def _extract_patches(x, patch_size, stride):
            n = (x.shape[1] - patch_size) // stride + 1
            idx = jnp.arange(n)[:, None] * stride + jnp.arange(patch_size)[None, :]
            w = x[:, idx, :]
            return w.reshape(x.shape[0], n, patch_size * x.shape[2])

        def _forward(x, W0, b0, pos0, W1, b1, pos1, W2, b2, pos2, scale_emb):
            params = [(W0, b0, pos0), (W1, b1, pos1), (W2, b2, pos2)]
            outs = []
            for i, (p, (W, b, pos)) in enumerate(zip(PATCH_SIZES, params)):
                s = max(1, int(p * STRIDE_RATIO))
                pt = _extract_patches(x, p, s)
                y = jnp.einsum('bnk,dk->bnd', pt, W) + b
                n = pt.shape[1]
                y = y + pos[:, :n, :] + scale_emb[i]
                outs.append(y)
            return jnp.concatenate(outs, axis=1)
        return _forward(x, W0, b0, pos0, W1, b1, pos1, W2, b2, pos2, scale_emb)

    def _L0_attn_ref(z, w_qkv, w_agg, b_agg):
        import jax, jax.numpy as jnp
        import numpy as np
        from math import sqrt
        bs, N, D = z.shape
        H = 8
        Dh = D // H
        qkv = jnp.einsum('bnd,ed->bne', z, w_qkv).reshape(bs, N, 3, H, Dh)
        q, k, v = jnp.moveaxis(qkv, 2, 0)
        q = q.transpose(0, 2, 1, 3)
        k = k.transpose(0, 2, 1, 3)
        v = v.transpose(0, 2, 1, 3)
        scores = jnp.einsum('bhnd,bhmd->bhnm', q, k) / sqrt(Dh)
        attn = jax.nn.softmax(scores, axis=-1)
        sa = jnp.einsum('bhnm,bhmd->bhnd', attn, v)
        sa = sa.transpose(0, 2, 1, 3).reshape(bs, N, H * Dh)
        out = jnp.einsum('bnd,ed->bne', sa, w_agg) + b_agg
        return out

    def _L0_ffn_ref(x, expert_weights, expert_indices, w1, w2):
        import jax, jax.numpy as jnp
        import numpy as np
        NUM_EXPERTS = 8
        TOP_K = 2
        'Dropless MoE: sort assignments by expert, gather tokens, grouped MLP,\n            scatter-combine with top-k router weights (megablocks gather/scatter semantics).'
        in_shape = x.shape
        hs = in_shape[-1]
        x_flat = x.reshape(-1, hs)
        T = x_flat.shape[0]
        flat_ids = expert_indices.reshape(-1)
        order = jnp.argsort(flat_ids)
        bin_ids = flat_ids[order]
        token_ids = order // TOP_K
        xg = x_flat[token_ids]
        y = jnp.zeros_like(xg)
        for e in range(NUM_EXPERTS):
            h = jax.nn.gelu(xg @ w1[e], approximate=False)
            y = jnp.where((bin_ids == e)[:, None], h @ w2[e], y)
        w = expert_weights.reshape(-1)[order][:, None]
        out = jnp.zeros((T, hs), x.dtype).at[token_ids].add(w * y)
        return out.reshape(in_shape)
    h = _L0_tok_ref(x, L0_tok_W0, L0_tok_b0, L0_tok_pos0, L0_tok_W1, L0_tok_b1, L0_tok_pos1, L0_tok_W2, L0_tok_b2, L0_tok_pos2, L0_tok_scale_emb)
    h = h + _L0_attn_ref(_layernorm(h, axis=-1), L0_attn_w_qkv, L0_attn_w_agg, L0_attn_b_agg)
    h = h + _L0_ffn_ref(_layernorm(h, axis=-1), L0_ffn_expert_weights, L0_ffn_expert_indices, L0_ffn_w1, L0_ffn_w2)
    return h

_drawn_inputs = setup_inputs


def setup_inputs(seed=0):
    import zlib

    import numpy as np

    out = dict(_drawn_inputs(seed))
    spreads = {}
    factors = {'L0_tok_b0': 3.687,
     'L0_tok_pos0': 6.07,
     'L0_tok_b1': 5.791,
     'L0_tok_pos1': 8.0,
     'L0_tok_b2': 8.0,
     'L0_tok_pos2': 8.0,
     'L0_attn_b_agg': 8.0}
    for name, (base, spread) in spreads.items():
        noise = np.random.default_rng([zlib.crc32(name.encode()), seed]).standard_normal(out[name].shape)
        drawn = base * np.exp(spread * noise) if base else spread * noise
        out[name] = jnp.asarray(drawn.astype(out[name].dtype))
    for name, factor in factors.items():
        out[name] = (out[name] * factor).astype(out[name].dtype)
    return out
```

```python
from contextlib import ExitStack

import concourse.bass as bass
from concourse import mybir

F32 = mybir.dt.float32
F32R = mybir.dt.float32r
I32 = mybir.dt.int32
U32 = mybir.dt.uint32
ALU = mybir.AluOpType
ACT = mybir.ActivationFunctionType
AX_X = mybir.AxisListType.X

P = 128
BATCH, CTX = 16, 512
PATCHES = (8, 16, 32)
N_SCALE = tuple((CTX - p) // (p // 2) + 1 for p in PATCHES)
N_AT = (0, N_SCALE[0], N_SCALE[0] + N_SCALE[1])
N = sum(N_SCALE)
N0, N1 = P, N - P
NE = N + 1
TAPS = sum(PATCHES)
TAP_AT = (0, PATCHES[0], PATCHES[0] + PATCHES[1])
R4 = 4
GROUP = 4
HEADS, DH = 8, 16
HALF = HEADS // 2
EPS = 1e-5
T_FFN, TOP_K, EXPERTS, FFN = 1024, 2, 8, 512
TJ = T_FFN // P
COLS = TJ * TOP_K
FC = FFN // P
N_TILES = T_FFN * TOP_K // P + EXPERTS - 1
TILE_N = (N0, N1)

C_IDENT, C_SEL, C_TRI, C_ONES, C_IOTA, C_THR, C_LT, C_TILE, C_KONE, C_END = (
    0, P, P + 16 * P, P + 17 * P, P + 18 * P, P + 19 * P, P + 20 * P, P + 20 * P + 64,
    P + 20 * P + 64 + N_TILES * EXPERTS, P + 20 * P + 64 + N_TILES * EXPERTS + 1)
MAX_ROW = 48


def build(nc, x, wt, pos, bias, wqkv, wagg, bagg, consts, ew, ei, w1, w2, out):
    with ExitStack() as ctx:
        def sb(name, shape, dt=F32):
            return ctx.enter_context(nc.sbuf_tensor(name, shape, dt))

        def sem(name):
            return ctx.enter_context(nc.semaphore(name))

        x_sb = sb("x_sb", [P, BATCH, R4, CTX // R4])
        wt_sb = sb("wt_sb", [P, TAPS, P])
        pos_sb = sb("pos_sb", [P, N])
        bias_sb = sb("bias_sb", [P, 6])
        comb = sb("comb", [P, N])
        wqkv_sb = sb("wqkv_sb", [P, 3 * P])
        wagg_sb = sb("wagg_sb", [P, P])
        bagg_sb = sb("bagg_sb", [P, P])
        c_sb = sb("c_sb", [P, C_END])
        sel_r = sb("sel_r", [P, 4, 4, P], F32R)
        ident_r = sb("ident_r", [P, P], F32R)
        hT = sb("hT", [P, GROUP, N])
        h_sb = sb("h_sb", [P, 2, P])
        hb = sb("hb", [P, 2, 2, P])
        stats = sb("stats", [P, 2, 6])
        counts = sb("counts", [P, 2])
        mv = sb("mv", [P, 2, 2])
        var_eps = sb("var_eps", [P, 2])
        rstd = sb("rstd", [P, 2])
        eps_t = sb("eps_t", [P, TJ])
        mhalf_t = sb("mhalf_t", [P, TJ])
        z_sb = sb("z_sb", [P, 2, P])
        zT = sb("zT", [P, N])
        qk_hi = sb("qk_hi", [P, 2, NE], F32R)
        qk_lo = sb("qk_lo", [P, 2, NE], F32R)
        v_aug = sb("v_aug", [P, 2, 2, HEADS, 32])
        q_st = sb("q_st", [P, HALF, NE], F32R)
        k_st = sb("k_st", [P, HALF, NE], F32R)
        nmax = sb("nmax", [P, 2, HALF, P], F32R)
        probs = sb("probs", [P, 2, 2, 2, 2, NE])
        o_raw = sb("o_raw", [P, 2, N])
        rden = sb("rden", [P, 2, HEADS])
        o_sb = sb("o_sb", [P, 2, P])
        o_T = sb("o_T", [P, N])
        h1 = sb("h1", [P, 2, 2, P])
        w1_sb = sb("w1_sb", [P, EXPERTS, FFN])
        w2_sb = sb("w2_sb", [P, EXPERTS, FC, P])
        ew_sb = sb("ew_sb", [P, TJ, TOP_K])
        ei_sb = sb("ei_sb", [P, TJ, TOP_K], I32)
        ei_f = sb("ei_f", [P, COLS])
        onehot = sb("onehot", [P, COLS, EXPERTS])
        before = sb("before", [P, COLS + 1, EXPERTS])
        rank = sb("rank", [P, COLS, EXPERTS])
        cmp_t = sb("cmp_t", [P, EXPERTS, 16])
        tiles_e = sb("tiles_e", [P, EXPERTS])
        lt_t = sb("lt_t", [P, EXPERTS, EXPERTS])
        base_e = sb("base_e", [P, EXPERTS])
        end_e = sb("end_e", [P, EXPERTS])
        base_s = sb("base_s", [P, EXPERTS])
        slot_f = sb("slot_f", [P, COLS])
        slot_u = sb("slot_u", [P, COLS], U32)
        te_t = sb("te_t", [P, N_TILES, EXPERTS])
        te_f = sb("te_f", [P, N_TILES])
        te_i = sb("te_i", [P, N_TILES], I32)
        zero = sb("zero", [P, P])
        h1m = sb("h1m", [P, TJ, P])
        stats2 = sb("stats2", [P, TJ, 6])
        mv2 = sb("mv2", [P, TJ, 2])
        var_eps2 = sb("var_eps2", [P, TJ])
        rstd2 = sb("rstd2", [P, TJ])
        z2 = sb("z2", [P, TJ, P])
        zs = sb("zs", [P, 2, P])
        zsT = sb("zsT", [P, 2, P])
        hid = sb("hid", [P, 2, FFN])
        hidT = sb("hidT", [P, 2, FC, P])
        y_sb = sb("y_sb", [P, 2, P])
        g_sb = sb("g_sb", [P, COLS, P])

        tok_ps = ctx.enter_context(nc.psum_tensor("tok_ps", [P, 2, 512], F32))
        s_ps = ctx.enter_context(nc.psum_tensor("s_ps", [P, 4, 512], F32))
        m_ps = ctx.enter_context(nc.psum_tensor("m_ps", [P, 2, 512], F32))

        z_dram = nc.dram_tensor("z_slots", (N_TILES * P, P), F32, kind="Internal").ap()
        y_dram = nc.dram_tensor("y_slots", (N_TILES * P, P), F32, kind="Internal").ap()

        ident = c_sb[:, C_IDENT:C_IDENT + P]
        out_rows = out.rearrange("b n d -> (b n) d")

        consts_in, small_in, idx_in = sem("consts_in"), sem("small_in"), sem("idx_in")
        x_in = [sem(f"x_in{g}") for g in range(BATCH // GROUP)]
        wt_in = [sem(f"wt_in{s}") for s in range(3)]
        w1_in, w2_in = sem("w1_in"), sem("w2_in")
        zero_set, z_cleared = sem("zero_set"), sem("z_cleared")
        pads_set, psum_set = sem("pads_set"), sem("psum_set")
        consts_r = sem("consts_r")
        comb_step, comb_ready = sem("comb_step"), sem("comb_ready")
        tok_done, hT_ready = sem("tok_done"), sem("hT_ready")
        h_turned, h_ready = sem("h_turned"), sem("h_ready")
        stats_ready, mv_ready = sem("stats_ready"), sem("mv_ready")
        eps_added, rstd_ready, hb_ready = sem("eps_added"), sem("rstd_ready"), sem("hb_ready")
        z_ready, z_turned, zT_ready = sem("z_ready"), sem("z_turned"), sem("zT_ready")
        qk_done, v_done = sem("qk_done"), sem("v_done")
        hi_ready, lo_ready, v_ready = sem("hi_ready"), sem("lo_ready"), sem("v_ready")
        stacked, q_st_ready, k_st_ready = sem("stacked"), sem("q_st_ready"), sem("k_st_ready")
        s1_done, max_ready = sem("s1_done"), sem("max_ready")
        max_placed, q_shifted = sem("max_placed"), sem("q_shifted")
        s2_done, probs_ready = sem("s2_done"), sem("probs_ready")
        pv_done, o_raw_ready, o_turned = sem("pv_done"), sem("o_raw_ready"), sem("o_turned")
        rden_ready, o_ready, on_turned, oT_ready = (
            sem("rden_ready"), sem("o_ready"), sem("on_turned"), sem("oT_ready"))
        agg_done, h1_ready = sem("agg_done"), sem("h1_ready")
        stored, h1_free = sem("stored"), sem("h1_free")
        route = sem("route")
        onehot_ready, counted = sem("onehot_ready"), sem("counted")
        routed = sem("routed")
        h1m_in, stats2_ready, mv2_ready = sem("h1m_in"), sem("stats2_ready"), sem("mv2_ready")
        eps2_added, rstd2_ready, z2_ready = sem("eps2_added"), sem("rstd2_ready"), sem("z2_ready")
        scattered = sem("scattered")
        zs_in = [sem("zs_in0"), sem("zs_in1")]
        zs_turned, zsT_ready = sem("zs_turned"), sem("zsT_ready")
        hid_done, hid_ready = sem("hid_done"), sem("hid_ready")
        hid_turned, hidT_ready = sem("hid_turned"), sem("hidT_ready")
        y_done, y_ready = sem("y_done"), sem("y_ready")
        y_out = [sem("y_out0"), sem("y_out1")]
        gathered = sem("gathered")
        combine = sem("combine")
        final_out = sem("final_out")

        block = ctx.enter_context(nc.Block())

        @block.sync
        def _(sp):
            def load_x(g):
                gs = slice(GROUP * g, GROUP * (g + 1))
                sp.dma_start(x_sb[:, gs], x[:, gs]).then_inc(x_in[g], 16)

            def load_wt(s):
                ts = slice(TAP_AT[s], TAP_AT[s] + PATCHES[s])
                sp.dma_start(wt_sb[:, ts], wt[:, ts]).then_inc(wt_in[s], 16)

            load_wt(0)
            load_x(0)
            sp.dma_start(c_sb[:], consts).then_inc(consts_in, 16)
            load_wt(1)
            load_wt(2)
            for dst, src in ((pos_sb, pos), (bias_sb, bias), (wqkv_sb, wqkv), (wagg_sb, wagg), (bagg_sb, bagg)):
                sp.dma_start(dst[:], src).then_inc(small_in, 16)
            sp.dma_start(ei_sb[:], ei.rearrange("(j p) k -> p j k", p=P)).then_inc(idx_in, 16)
            sp.dma_start(ew_sb[:], ew.rearrange("(j p) k -> p j k", p=P)).then_inc(idx_in, 16)
            load_x(1)
            load_x(2)
            load_x(3)
            sp.dma_start(w1_sb[:], w1.rearrange("e h f -> h e f")).then_inc(w1_in, 16)
            sp.dma_start(w2_sb[:], w2.rearrange("e (c p) d -> p e c d", p=P)).then_inc(w2_in, 16)
            sp.wait_ge(zero_set, 1)
            sp.dma_start(z_dram.rearrange("(i p) d -> p i d", p=P),
                         zero[:].unsqueeze(1).to_broadcast([P, N_TILES, P])).then_inc(z_cleared, 16)

            def store_h1(b, par):
                sp.wait_ge(h1_ready, b + 1)
                sp.dma_start(out[bass.ds(b, 1), 0:N0, :].squeeze(0) if not isinstance(b, int) else out[b, 0:N0, :],
                             h1[:, par, 0, :]).then_inc(stored, 16)
                sp.dma_start(out[bass.ds(b, 1), N0:N, :].squeeze(0) if not isinstance(b, int) else out[b, N0:N, :],
                             h1[0:N1, par, 1, :]).then_inc(stored, 16)
                sp.wait_ge(stored, b * 32 + 32)
                sp.sem_inc(h1_free, 1)

            with sp.Fori(0, BATCH // 2) as i:
                for par in range(2):
                    store_h1(i * 2 + par, par)

            sp.dma_start(h1m[:], out_rows[0:T_FFN].rearrange("(j p) d -> p j d", p=P)).then_inc(h1m_in, 16)
            sp.wait_ge(scattered, 16 * COLS)

            def load_zs(i, par):
                sp.dma_start(zs[:, par, :], z_dram[bass.ds(i * P, P), :]).then_inc(zs_in[par], 16)

            def store_y(i, par):
                sp.wait_ge(y_ready, i + 1)
                sp.dma_start(y_dram[bass.ds(i * P, P), :], y_sb[:, par, :]).then_inc(y_out[par], 16)

            load_zs(0, 0)
            load_zs(1, 1)

            def step(i, par, more):
                if more:
                    sp.wait_ge(zs_turned, i + 1)
                    load_zs(i + 2, par)
                store_y(i, par)

            with sp.Fori(0, (N_TILES - 3) // 2) as k:
                for par in range(2):
                    step(k * 2 + par, par, True)
            step(N_TILES - 3, (N_TILES - 3) % 2, True)
            step(N_TILES - 2, (N_TILES - 2) % 2, False)
            step(N_TILES - 1, (N_TILES - 1) % 2, False)
            sp.wait_ge(combine, COLS)
            sp.dma_start(out_rows[0:T_FFN].rearrange("(j p) d -> p j d", p=P), h1m[:]).then_inc(final_out, 16)
            sp.wait_ge(final_out, 16)

        @block.gpsimd
        def _(pool):
            g = nc.gpsimd
            g.memset(zero[:], 0.0).then_inc(zero_set, 1)
            pool.sem_inc(h1_free, 2)
            g.memset(eps_t[:], EPS)
            g.memset(mhalf_t[:], -0.5)
            g.memset(qk_hi[:, :, N:NE].bitcast(F32), 0.0)
            g.memset(qk_lo[:, :, N:NE].bitcast(F32), 0.0)
            g.memset(nmax[:].bitcast(F32), 0.0)
            g.memset(v_aug[:], 0.0).then_inc(pads_set, 1)
            pool.wait_ge(pads_set, 1)
            g.memset(v_aug[:, :, :, :, DH:DH + 1], 1.0).then_inc(pads_set, 1)

            def stage1(b, par):
                pool.wait_ge(mv_ready, b * 2 + 2)
                g.tensor_tensor(var_eps[:], mv[:, :, 1], eps_t[:, 0:2], ALU.add).then_inc(eps_added, 1)
                pool.wait_ge(eps_added, b + 1)
                g.tensor_tensor(rstd[:], var_eps[:], mhalf_t[:, 0:2], ALU.pow).then_inc(rstd_ready, 1)
                pool.wait_ge(h_ready, b + 1)
                g.tensor_tensor(hb[:, par], h_sb[:], bagg_sb[:].unsqueeze(1).to_broadcast([P, 2, P]),
                                ALU.add).then_inc(hb_ready, 1)

            pool.wait_ge(small_in, 16 * 5)
            with pool.Fori(0, BATCH // 2) as i:
                for par in range(2):
                    stage1(i * 2 + par, par)

            pool.wait_ge(mv2_ready, TJ)
            g.tensor_tensor(var_eps2[:], mv2[:, :, 1], eps_t[:], ALU.add).then_inc(eps2_added, 1)
            pool.wait_ge(eps2_added, 1)
            g.tensor_tensor(rstd2[:], var_eps2[:], mhalf_t[:], ALU.pow).then_inc(rstd2_ready, 1)
            pool.wait_ge(routed, 1)
            pool.wait_ge(z_cleared, 16)
            for j in range(TJ):
                pool.wait_ge(z2_ready, j + 1)
                for k in range(TOP_K):
                    c = j * TOP_K + k
                    g.indirect_dma_start(
                        z_dram, bass.IndirectOffsetOnAxis(ap=slot_u[:, c:c + 1], axis=0),
                        z2[:, j, :], None).then_inc(scattered, 16)
            for par in range(2):
                pool.wait_ge(y_out[par], 16 * ((N_TILES + 1 - par) // 2))
            for c in range(COLS):
                g.indirect_dma_start(
                    g_sb[:, c, :], None, y_dram,
                    bass.IndirectOffsetOnAxis(ap=slot_u[:, c:c + 1], axis=0)).then_inc(gathered, 16)

        @block.scalar
        def _(act):
            s = nc.scalar

            def stage1_head(b, first=False):
                if not first:
                    act.wait_ge(hb_ready, b)
                act.wait_ge(h_turned, b + 1)
                s.copy(h_sb[:], m_ps[:, 0, 0:2 * P].rearrange("p (t d) -> p t d", t=2)).then_inc(h_ready, 1)

            def stage1_zT(b):
                act.wait_ge(z_turned, b + 1)
                s.copy(zT[:], m_ps[:, 1, 0:N]).then_inc(zT_ready, 1)

            def stage1_hi(b):
                act.wait_ge(qk_done, b + 1)
                s.copy(qk_hi[:, :, 0:N], m_ps[:, 0, 0:2 * N].rearrange("p (w n) -> p w n", w=2)).then_inc(hi_ready, 1)

            def stage1_v(b, par):
                act.wait_ge(v_done, b + 1)
                s.copy(v_aug[:, par, :, :, 0:DH],
                       m_ps[:, 1, 0:2 * P].rearrange("p (t h d) -> p t h d", t=2, h=HEADS)).then_inc(v_ready, 1)

            def stage1_stack(b):
                act.wait_ge(stacked, b * 2 + 1)
                s.copy(q_st[:].rearrange("p (a j) n -> p a (j n)", a=2), s_ps[:, 0:2, 0:2 * NE]).then_inc(q_st_ready, 1)
                act.wait_ge(stacked, b * 2 + 2)
                s.activation(k_st[:].rearrange("p (a j) n -> p a (j n)", a=2), s_ps[:, 2:4, 0:2 * NE],
                             ACT.Identity, bias=c_sb[:, C_KONE:C_KONE + 1]).then_inc(k_st_ready, 1)

            def exps(b, t):
                for f in range(2):
                    act.wait_ge(s2_done, b * 4 + (2 * t + f + 1))
                    n = TILE_N[t]
                    s.activation(probs[0:n, t, f].rearrange("p r j n -> p r (j n)"),
                                 s_ps[0:n, 2 * f:2 * f + 2, 0:2 * NE], ACT.Exp,
                                 scale=DH ** -0.5).then_inc(probs_ready, 1)

            def stage2_oraw(b):
                act.wait_ge(pv_done, b + 1)
                s.copy(o_raw[:], m_ps[:, 0, 0:2 * N].rearrange("p (r n) -> p r n", r=2)).then_inc(o_raw_ready, 1)

            def stage2_oT(b):
                act.wait_ge(on_turned, b + 1)
                s.copy(o_T[:], m_ps[:, 0, 0:N]).then_inc(oT_ready, 1)

            def stage1(b, par):
                stage1_head(b, True)
                stage1_zT(b)
                stage1_hi(b)
                stage1_v(b, par)
                stage1_stack(b)

            def slot(b, par):
                stage1_head(b + 1)
                stage1_zT(b + 1)
                exps(b, 0)
                stage1_hi(b + 1)
                exps(b, 1)
                stage1_v(b + 1, 1 - par)
                stage2_oraw(b)
                stage1_stack(b + 1)
                stage2_oT(b)

            act.wait_ge(pads_set, 2)
            act.wait_ge(consts_in, 16)
            stage1(0, 0)
            with act.Fori(0, BATCH // GROUP - 1) as g:
                for j in range(GROUP):
                    slot(g * GROUP + j, j % 2)
            for b in range(BATCH - GROUP, BATCH - 1):
                slot(b, b % 2)
            exps(BATCH - 1, 0)
            exps(BATCH - 1, 1)
            stage2_oraw(BATCH - 1)
            stage2_oT(BATCH - 1)

            def gelu(i, par):
                act.wait_ge(hid_done, i + 1)
                s.activation(hid[:, par, :], s_ps[:, par, :], ACT.Gelu).then_inc(hid_ready, 1)

            with act.Fori(0, N_TILES // 2) as k:
                for par in range(2):
                    gelu(k * 2 + par, par)
            gelu(N_TILES - 1, (N_TILES - 1) % 2)

        @block.vector
        def _(dve):
            v = nc.vector
            v.memset(m_ps[:], 0.0).then_inc(psum_set, 1)
            dve.wait_ge(consts_in, 16)
            v.tensor_copy(ident_r[:], ident).then_inc(consts_r, 1)
            v.tensor_copy(sel_r[:].rearrange("p a j m -> p (a j m)"),
                          c_sb[:, C_SEL:C_SEL + 16 * P]).then_inc(consts_r, 1)
            dve.wait_ge(small_in, 16 * 5)
            for i in range(3):
                v.tensor_scalar(comb[:, N_AT[i]:N_AT[i] + N_SCALE[i]], pos_sb[:, N_AT[i]:N_AT[i] + N_SCALE[i]],
                                bias_sb[:, i:i + 1], bias_sb[:, 3 + i:4 + i], ALU.add, ALU.add).then_inc(comb_ready, 1)
            dve.wait_ge(comb_ready, 3)

            steps = [0]

            def link(ins):
                steps[0] += 1
                ins.then_inc(route, 1)
                dve.wait_ge(route, steps[0])

            dve.wait_ge(idx_in, 32)
            link(v.tensor_copy(ei_f[:], ei_sb[:].rearrange("p j k -> p (j k)")))
            v.tensor_tensor(onehot[:], ei_f[:].unsqueeze(2).to_broadcast([P, COLS, EXPERTS]),
                            c_sb[:, C_IOTA:C_IOTA + P].rearrange("p (c e) -> p c e", e=EXPERTS),
                            ALU.is_equal).then_inc(onehot_ready, 1)
            link(v.memset(before[:, 0, :], 0.0))
            dve.wait_ge(counted, 2)
            for c in range(COLS):
                link(v.tensor_tensor(before[:, c + 1, :], before[:, c, :],
                                     s_ps[:, 1, c * EXPERTS:(c + 1) * EXPERTS], ALU.add))
            total = before[:, COLS, :]
            link(v.tensor_tensor(cmp_t[:], total.unsqueeze(2).to_broadcast([P, EXPERTS, 16]),
                                 c_sb[:, C_THR:C_THR + P].rearrange("p (e m) -> p e m", m=16), ALU.is_gt))
            link(v.tensor_reduce(tiles_e[:], cmp_t[:], AX_X, ALU.add))
            link(v.tensor_tensor(lt_t[:], tiles_e[:].unsqueeze(1).to_broadcast([P, EXPERTS, EXPERTS]),
                                 c_sb[:, C_LT:C_LT + 64].rearrange("p (e f) -> p e f", f=EXPERTS), ALU.mult))
            link(v.tensor_reduce(base_e[:], lt_t[:], AX_X, ALU.add))
            link(v.tensor_tensor(end_e[:], base_e[:], tiles_e[:], ALU.add))
            link(v.tensor_scalar(base_s[:], base_e[:], float(P), None, ALU.mult))
            link(v.tensor_tensor(rank[:], before[:, 0:COLS, :],
                                 s_ps[:, 0, 0:P].rearrange("p (c e) -> p c e", e=EXPERTS), ALU.add))
            link(v.tensor_tensor(rank[:], rank[:], base_s[:].unsqueeze(1).to_broadcast([P, COLS, EXPERTS]), ALU.add))
            link(v.tensor_tensor(rank[:], rank[:], onehot[:], ALU.mult))
            link(v.tensor_reduce(slot_f[:], rank[:], AX_X, ALU.add))
            link(v.tensor_copy(slot_u[:], slot_f[:]))
            link(v.tensor_tensor(te_t[:], end_e[:].unsqueeze(1).to_broadcast([P, N_TILES, EXPERTS]),
                                 c_sb[:, C_TILE:C_TILE + N_TILES * EXPERTS].rearrange("p (i e) -> p i e", e=EXPERTS),
                                 ALU.is_le))
            link(v.tensor_reduce(te_f[:], te_t[:], AX_X, ALU.add))
            v.tensor_scalar(te_i[:], te_f[:], float(EXPERTS - 1), None, ALU.min).then_inc(routed, 1)

            def hT_evac(g):
                dve.wait_ge(tok_done, g * 3 + 3)
                for i, src in enumerate((tok_ps[:, 0, 0:GROUP * N_SCALE[0]],
                                         tok_ps[:, 1, 0:GROUP * N_SCALE[1]],
                                         tok_ps[:, 1, GROUP * N_SCALE[1]:GROUP * (N_SCALE[1] + N_SCALE[2])])):
                    a, n = N_AT[i], N_SCALE[i]
                    v.tensor_tensor(hT[:, :, a:a + n], src.rearrange("p (b n) -> p b n", b=GROUP),
                                    comb[:, a:a + n].unsqueeze(1).to_broadcast([P, GROUP, n]),
                                    ALU.add).then_inc(hT_ready, 1)

            def stage1_stats(b):
                dve.wait_ge(h_ready, b + 1)
                for t in range(2):
                    v.bn_stats(stats[:, t, :], h_sb[:, t, :]).then_inc(stats_ready, 1)
                dve.wait_ge(stats_ready, b * 2 + 2)
                v.tensor_copy(counts[:], stats[:, :, 0])
                for t in range(2):
                    v.bn_aggr(mv[:, t, :], stats[:, t, :]).then_inc(mv_ready, 1)

            def stage1_z(b):
                dve.wait_ge(rstd_ready, b + 1)
                for t in range(2):
                    v.tensor_scalar(z_sb[:, t, :], h_sb[:, t, :], mv[:, t, 0:1], rstd[:, t:t + 1],
                                    ALU.subtract, ALU.mult).then_inc(z_ready, 1)

            def stage1_lo(b):
                dve.wait_ge(hi_ready, b + 1)
                v.tensor_tensor(qk_lo[:, :, 0:N], m_ps[:, 0, 0:2 * N].rearrange("p (w n) -> p w n", w=2),
                                qk_hi[:, :, 0:N].bitcast(F32), ALU.subtract).then_inc(lo_ready, 1)

            def stage1_max(b, t):
                n = TILE_N[t]
                for f in range(2):
                    dve.wait_ge(s1_done, b * 4 + (2 * t + f + 1))
                    dst = nmax[0:n, t, 2 * f:2 * f + 2, :].rearrange("p j (r m) -> p r j m", r=2)[:, :, :, MAX_ROW]
                    src = s_ps[0:n, 2 * f:2 * f + 2, 0:2 * NE].rearrange("p r (j n) -> p r j n", j=2)[:, :, :, 0:N]
                    v.tensor_reduce(dst, src, AX_X, ALU.max, negate=True).then_inc(max_ready, 1)

            def stage2_shift(b):
                dve.wait_ge(max_placed, b + 1)
                qv = q_st[:].rearrange("p (a j) n -> p a (j n)", a=2)
                v.tensor_tensor(qv, s_ps[:, 0:2, 0:2 * NE], qv.bitcast(F32), ALU.add).then_inc(q_shifted, 1)

            def stage2_norm(b):
                dve.wait_ge(o_turned, b + 1)
                for t in range(2):
                    n = TILE_N[t]
                    o = m_ps[0:n, 1, 256 * t:256 * (t + 1)].rearrange("p (h e) -> p h e", e=32)
                    v.reciprocal(rden[0:n, t, :], o[:, :, DH]).then_inc(rden_ready, 1)
                dve.wait_ge(rden_ready, b * 2 + 2)
                for t in range(2):
                    n = TILE_N[t]
                    o = m_ps[0:n, 1, 256 * t:256 * (t + 1)].rearrange("p (h e) -> p h e", e=32)
                    v.tensor_tensor(o_sb[0:n, t, :].rearrange("p (h d) -> p h d", d=DH), o[:, :, 0:DH],
                                    rden[0:n, t, :].unsqueeze(2).to_broadcast([n, HEADS, DH]),
                                    ALU.mult).then_inc(o_ready, 1)

            def stage2_h1(b, par):
                dve.wait_ge(agg_done, b + 1)
                dve.wait_ge(hb_ready, b + 1)
                dve.wait_ge(h1_free, b + 1)
                v.tensor_tensor(h1[:, par], m_ps[:, 1, 0:2 * P].rearrange("p (t d) -> p t d", t=2),
                                hb[:, par], ALU.add).then_inc(h1_ready, 1)

            def stage1(b):
                stage1_stats(b)
                stage1_z(b)
                stage1_lo(b)
                stage1_max(b, 0)
                stage1_max(b, 1)

            def slot(b, par, j, g=None):
                if j == GROUP - 1 and g is not None:
                    hT_evac(g + 1)
                stage1_stats(b + 1)
                stage2_shift(b)
                stage1_z(b + 1)
                stage1_lo(b + 1)
                stage2_norm(b)
                stage1_max(b + 1, 0)
                stage1_max(b + 1, 1)
                stage2_h1(b, par)

            hT_evac(0)
            stage1(0)
            with dve.Fori(0, BATCH // GROUP - 1) as g:
                for j in range(GROUP):
                    slot(g * GROUP + j, j % 2, j, g)
            for b in range(BATCH - GROUP, BATCH - 1):
                slot(b, b % 2, 0)
            stage2_shift(BATCH - 1)
            stage2_norm(BATCH - 1)
            stage2_h1(BATCH - 1, 1)

            dve.wait_ge(h1m_in, 16)
            for j in range(TJ):
                v.bn_stats(stats2[:, j, :], h1m[:, j, :]).then_inc(stats2_ready, 1)
            for j in range(TJ):
                dve.wait_ge(stats2_ready, j + 1)
                v.bn_aggr(mv2[:, j, :], stats2[:, j, :]).then_inc(mv2_ready, 1)
            dve.wait_ge(rstd2_ready, 1)
            for j in range(TJ):
                v.tensor_scalar(z2[:, j, :], h1m[:, j, :], mv2[:, j, 0:1], rstd2[:, j:j + 1],
                                ALU.subtract, ALU.mult).then_inc(z2_ready, 1)

            def zsT_evac(i, par):
                dve.wait_ge(zs_turned, i + 1)
                v.tensor_copy(zsT[:, par, :], m_ps[:, 0, 0:P]).then_inc(zsT_ready, 1)

            def hidT_evac(i, par):
                dve.wait_ge(hid_turned, i + 1)
                v.tensor_copy(hidT[:, par].rearrange("p c s -> p (c s)"), s_ps[:, 2 + par, :]).then_inc(hidT_ready, 1)

            def y_evac(i, par, old=True):
                dve.wait_ge(y_done, i + 1)
                if old:
                    dve.wait_ge(y_out[par], (i - par) * 8)
                v.tensor_copy(y_sb[:, par, :], m_ps[:, 1, 0:P]).then_inc(y_ready, 1)

            def step(i, par, more_z, more_h, old=True):
                if more_z:
                    zsT_evac(i + 2, par)
                y_evac(i, par, old)
                if more_h:
                    hidT_evac(i + 1, 1 - par)

            zsT_evac(0, 0)
            zsT_evac(1, 1)
            hidT_evac(0, 0)
            step(0, 0, True, True, False)
            step(1, 1, True, True, False)
            with dve.Fori(1, (N_TILES - 3) // 2) as k:
                for par in range(2):
                    step(k * 2 + par, par, True, True)
            step(N_TILES - 3, (N_TILES - 3) % 2, True, True)
            step(N_TILES - 2, (N_TILES - 2) % 2, False, True)
            step(N_TILES - 1, (N_TILES - 1) % 2, False, False)
            dve.wait_ge(gathered, 16 * COLS)
            for k in range(TOP_K):
                if k:
                    dve.wait_ge(combine, TJ)
                for j in range(TJ):
                    v.scalar_tensor_tensor(out=h1m[:, j, :], in0=g_sb[:, j * TOP_K + k, :],
                                           scalar=ew_sb[:, j, k:k + 1], in1=h1m[:, j, :],
                                           op0=ALU.mult, op1=ALU.add).then_inc(combine, 1)

        @block.tensor
        def _(pe):
            def tok(g, lo, hi):
                for c in range(lo, hi):
                    i = 0 if c < TAP_AT[1] else 1 if c < TAP_AT[2] else 2
                    t = c - TAP_AT[i]
                    st = PATCHES[i] // 2 // R4
                    q0, n = t // R4, N_SCALE[i]
                    xs = x_sb[:, bass.ds(g * GROUP, GROUP), t % R4, q0:q0 + (n - 1) * st + 1:st]
                    o0 = 0 if i < 2 else GROUP * N_SCALE[1]
                    dst = tok_ps[:, min(i, 1), o0:o0 + GROUP * n].rearrange("p (b n) -> p b n", b=GROUP)
                    mm = pe.matmul(dst, wt_sb[:, c, :], xs, start=(t == 0), stop=(t == PATCHES[i] - 1))
                    if t == PATCHES[i] - 1:
                        mm.then_inc(tok_done, 1)

            def h_turn(b, j, g=None):
                if g is not None:
                    pe.wait_ge(hT_ready, g * 3 + 3)
                pe.transpose(m_ps[:, 0, 0:P], hT[:, j, 0:N0], ident)
                pe.transpose(m_ps[0:N1, 0, P:2 * P], hT[:, j, N0:N], ident).then_inc(h_turned, 1)

            def z_turn(b):
                pe.wait_ge(z_ready, b * 2 + 2)
                pe.transpose(m_ps[:, 1, 0:N0], z_sb[:, 0, :], ident)
                pe.transpose(m_ps[:, 1, N0:N], z_sb[0:N1, 1, :], ident[0:N1, 0:N1]).then_inc(z_turned, 1)

            def project(b):
                pe.wait_ge(zT_ready, b + 1)
                for w in range(2):
                    mm = pe.matmul(m_ps[:, 0, w * N:(w + 1) * N], wqkv_sb[:, w * P:(w + 1) * P], zT[:],
                                   start=True, stop=True)
                mm.then_inc(qk_done, 1)
                pe.matmul(m_ps[:, 1, 0:P], zT[:, 0:N0], wqkv_sb[:, 2 * P:3 * P], start=True, stop=True)
                pe.matmul(m_ps[0:N1, 1, P:2 * P], zT[:, N0:N], wqkv_sb[:, 2 * P:3 * P],
                          start=True, stop=True).then_inc(v_done, 1)

            def stack(b):
                pe.wait_ge(lo_ready, b + 1)
                for w in range(2):
                    for j in range(HALF):
                        dst = s_ps[:, 2 * w + j // 2, (j % 2) * NE:(j % 2 + 1) * NE]
                        pe.matmul(dst, sel_r[:, 2 * w, j, :], qk_hi[:, w, :], start=True, stop=False)
                        mm = pe.matmul(dst, sel_r[:, 2 * w + 1, j, :], qk_lo[:, w, :], start=False, stop=True)
                    mm.then_inc(stacked, 1)

            def scores(a, bb, t, f, done):
                n = TILE_N[t]
                for jj in range(2):
                    for r in range(2):
                        j = 2 * f + jj
                        mm = pe.matmul(s_ps[0:n, 2 * f + r, jj * NE:(jj + 1) * NE],
                                       a[64 * r:64 * r + 64, j, P * t:P * t + n], bb[64 * r:64 * r + 64, j, :],
                                       start=True, stop=True)
                mm.then_inc(done, 1)

            def s1(b, t):
                for f in range(2):
                    if t == 0 and f == 0:
                        pe.wait_ge(q_st_ready, b + 1)
                        pe.wait_ge(k_st_ready, b + 1)
                    if t == 1:
                        pe.wait_ge(max_ready, b * 4 + f + 1)
                    scores(q_st, k_st, t, f, s1_done)

            def place_max(b):
                pe.wait_ge(max_ready, b * 4 + 4)
                for j in range(HALF):
                    for t in range(2):
                        n = TILE_N[t]
                        w = P if t == 0 else NE - P
                        o = (j % 2) * NE + P * t
                        mm = pe.matmul(s_ps[:, j // 2, o:o + w], nmax[0:n, t, j, :], ident_r[0:n, 0:w],
                                       start=True, stop=True)
                mm.then_inc(max_placed, 1)

            def s2(b, t):
                for f in range(2):
                    if t == 0 and f == 0:
                        pe.wait_ge(q_shifted, b + 1)
                    if t == 1:
                        pe.wait_ge(probs_ready, b * 4 + f + 1)
                    scores(k_st, q_st, t, f, s2_done)

            def pv(b, par, last=False):
                pe.wait_ge(probs_ready, b * 4 + 4)
                if not last:
                    pe.wait_ge(lo_ready, b + 2)
                for r in range(2):
                    for t in range(2):
                        n = TILE_N[t]
                        for j in range(HALF):
                            mm = pe.matmul(m_ps[32 * j:32 * j + 32, 0, r * N:(r + 1) * N],
                                           v_aug[0:n, par, t, HALF * r + j, :],
                                           probs[0:n, t, j // 2, r, j % 2, 0:N],
                                           start=(t == 0), stop=(t == 1))
                mm.then_inc(pv_done, 1)

            def o_turn(b):
                pe.wait_ge(o_raw_ready, b + 1)
                for t in range(2):
                    n = TILE_N[t]
                    for r in range(2):
                        mm = pe.transpose(m_ps[0:n, 1, 256 * t + P * r:256 * t + P * (r + 1)],
                                          o_raw[:, r, P * t:P * t + n], ident)
                mm.then_inc(o_turned, 1)

            def on_turn(b):
                pe.wait_ge(o_ready, b * 2 + 2)
                pe.transpose(m_ps[:, 0, 0:N0], o_sb[:, 0, :], ident)
                pe.transpose(m_ps[:, 0, N0:N], o_sb[0:N1, 1, :], ident[0:N1, 0:N1]).then_inc(on_turned, 1)

            def aggregate(b):
                pe.wait_ge(oT_ready, b + 1)
                pe.matmul(m_ps[:, 1, 0:P], o_T[:, 0:N0], wagg_sb[:], start=True, stop=True)
                pe.matmul(m_ps[0:N1, 1, P:2 * P], o_T[:, N0:N], wagg_sb[:], start=True,
                          stop=True).then_inc(agg_done, 1)

            pe.wait_ge(x_in[0], 16)
            pe.wait_ge(wt_in[0], 16)
            tok(0, 0, TAP_AT[1])
            pe.wait_ge(consts_in, 16)
            pe.wait_ge(onehot_ready, 1)
            oh = onehot[:].rearrange("p c e -> p (c e)")
            pe.matmul(s_ps[:, 0, 0:P], c_sb[:, C_TRI:C_TRI + P], oh, start=True, stop=True).then_inc(counted, 1)
            pe.matmul(s_ps[:, 1, 0:P], c_sb[:, C_ONES:C_ONES + P], oh, start=True, stop=True).then_inc(counted, 1)
            pe.wait_ge(wt_in[1], 16)
            tok(0, TAP_AT[1], TAP_AT[2])
            pe.wait_ge(wt_in[2], 16)
            tok(0, TAP_AT[2], TAPS)
            pe.wait_ge(psum_set, 1)
            h_turn(0, 0, 0)
            z_turn(0)
            pe.wait_ge(small_in, 16 * 5)
            project(0)
            pe.wait_ge(consts_r, 2)
            pe.wait_ge(routed, 1)
            stack(0)
            s1(0, 0)
            s1(0, 1)
            for q in x_in[1:]:
                pe.wait_ge(q, 16)

            SHARE = (0, 16, 32, 48, TAPS)

            def slot(b, par, j, g=None):
                chunks = list(range(SHARE[j], SHARE[j + 1])) if g is not None else []
                k = [0]

                def fill(n):
                    if chunks:
                        lo = chunks[0] + k[0]
                        hi = min(lo + n, chunks[-1] + 1)
                        if hi > lo:
                            tok(g + 1, lo, hi)
                            k[0] += hi - lo

                m = len(chunks)
                nxt = (j + 1) % GROUP
                if j == GROUP - 1:
                    fill(m)
                h_turn(b + 1, nxt, g + 1 if (j == GROUP - 1 and g is not None) else None)
                fill(m // 8)
                place_max(b)
                fill(m // 4)
                z_turn(b + 1)
                s2(b, 0)
                project(b + 1)
                fill(m // 8)
                s2(b, 1)
                fill(m // 4)
                pv(b, par)
                stack(b + 1)
                o_turn(b)
                fill(m // 8)
                s1(b + 1, 0)
                on_turn(b)
                fill(m)
                s1(b + 1, 1)
                aggregate(b)

            with pe.Fori(0, BATCH // GROUP - 1) as g:
                for j in range(GROUP):
                    slot(g * GROUP + j, j % 2, j, g)
            for j in range(GROUP - 1):
                slot(BATCH - GROUP + j, j % 2, j)
            b = BATCH - 1
            place_max(b)
            s2(b, 0)
            s2(b, 1)
            pv(b, 1, last=True)
            o_turn(b)
            on_turn(b)
            aggregate(b)

            def zs_turn(i, par, n_in):
                pe.wait_ge(zs_in[par], n_in)
                pe.transpose(m_ps[:, 0, 0:P], zs[:, par, :], ident).then_inc(zs_turned, 1)

            def hidden(i, par):
                e = pe.value_load(te_i[0:1, bass.ds(i, 1)], min_val=0, max_val=EXPERTS - 1)
                pe.wait_ge(zsT_ready, i + 1)
                pe.matmul(s_ps[:, par, :], zsT[:, par, :], w1_sb[:, bass.ds(e, 1), :].rearrange("p a f -> p (a f)"),
                          start=True, stop=True).then_inc(hid_done, 1)

            def hid_turn(i, par):
                pe.wait_ge(hid_ready, i + 1)
                for c in range(FC):
                    mm = pe.transpose(s_ps[:, 2 + par, c * P:(c + 1) * P], hid[:, par, c * P:(c + 1) * P], ident)
                mm.then_inc(hid_turned, 1)

            def down(i, par):
                e = pe.value_load(te_i[0:1, bass.ds(i, 1)], min_val=0, max_val=EXPERTS - 1)
                pe.wait_ge(hidT_ready, i + 1)
                for c in range(FC):
                    mm = pe.matmul(m_ps[:, 1, 0:P], hidT[:, par, c, :],
                                   w2_sb[:, bass.ds(e, 1), c, :].rearrange("p a d -> p (a d)"),
                                   start=(c == 0), stop=(c == FC - 1))
                mm.then_inc(y_done, 1)

            def step(i, par, more_z, more_h, prev=True):
                if more_z:
                    zs_turn(i + 2, par, (i - par) * 8 + 32)
                if prev:
                    pe.wait_ge(y_ready, i)
                down(i, par)
                if more_h:
                    hid_turn(i + 1, 1 - par)
                if more_z:
                    hidden(i + 2, par)

            pe.wait_ge(w1_in, 16)
            pe.wait_ge(w2_in, 16)
            pe.wait_ge(h1_ready, BATCH)
            zs_turn(0, 0, 16)
            hidden(0, 0)
            zs_turn(1, 1, 16)
            hid_turn(0, 0)
            hidden(1, 1)
            with pe.Fori(0, (N_TILES - 3) // 2) as k:
                for par in range(2):
                    step(k * 2 + par, par, True, True)
            step(N_TILES - 3, (N_TILES - 3) % 2, True, True)
            step(N_TILES - 2, (N_TILES - 2) % 2, False, True)
            step(N_TILES - 1, (N_TILES - 1) % 2, False, False)


def constants(np):
    c = np.zeros((P, C_END), np.float32)
    c[:, C_IDENT:C_IDENT + P] = np.eye(P)
    sel = np.zeros((P, 4, HALF, P), np.float32)
    for r in range(2):
        for j in range(HALF):
            for d in range(DH):
                src = (HALF * r + j) * DH + d
                row = 64 * r + d
                for which, blocks in enumerate(((0, 1), (2,), (0, 2), (1,))):
                    for blk in blocks:
                        sel[src, which, j, row + DH * blk] = 1.0
    c[:, C_SEL:C_SEL + 16 * P] = sel.reshape(P, -1)
    c[:, C_TRI:C_TRI + P] = np.triu(np.ones((P, P)), 1)
    c[:, C_ONES:C_ONES + P] = 1.0
    c[:, C_IOTA:C_IOTA + P] = np.tile(np.arange(EXPERTS), COLS)
    c[:, C_THR:C_THR + P] = np.tile(np.arange(16) * P, EXPERTS)
    c[:, C_LT:C_LT + 64] = np.tril(np.ones((EXPERTS, EXPERTS)), -1).reshape(-1)
    c[:, C_TILE:C_TILE + N_TILES * EXPERTS] = np.repeat(np.arange(N_TILES), EXPERTS)
    c[MAX_ROW, C_KONE] = c[64 + MAX_ROW, C_KONE] = 1.0
    return c


def kernel(**inputs):
    import numpy as np
    import concourse.bacc as bacc
    from concourse.bass_utils import run_bass_kernel_spmd

    a = {k: np.asarray(v) for k, v in inputs.items()}
    arrays = {
        "x": a["x"].transpose(2, 0, 1).reshape(P, BATCH, CTX // R4, R4).transpose(0, 1, 3, 2),
        "wt": np.concatenate([a[f"L0_tok_W{i}"].reshape(P, p, P).transpose(2, 1, 0)
                              for i, p in enumerate(PATCHES)], axis=1),
        "pos": np.concatenate([a[f"L0_tok_pos{i}"][0] for i in range(3)], axis=0).T,
        "bias": np.stack([a[f"L0_tok_b{i}"] for i in range(3)]
                         + [a["L0_tok_scale_emb"][i] for i in range(3)], axis=1),
        "wqkv": a["L0_attn_w_qkv"].T,
        "wagg": a["L0_attn_w_agg"].T,
        "bagg": np.broadcast_to(a["L0_attn_b_agg"][None, :], (P, P)),
        "consts": constants(np),
        "ew": a["L0_ffn_expert_weights"],
        "ei": a["L0_ffn_expert_indices"],
        "w1": a["L0_ffn_w1"],
        "w2": a["L0_ffn_w2"],
    }
    arrays = {k: np.ascontiguousarray(v) for k, v in arrays.items()}
    nc = bacc.Bacc("TRN2", target_bir_lowering=False, num_devices=1)
    aps = [nc.dram_tensor(k, v.shape, mybir.dt.from_np(v.dtype), kind="ExternalInput").ap() for k, v in arrays.items()]
    out = nc.dram_tensor("out", (BATCH, N, P), F32, kind="ExternalOutput").ap()
    build(nc, *aps, out)
    r = run_bass_kernel_spmd(nc, [arrays], core_ids=[0])
    return r.results[0]["out"]
```

```python
from contextlib import ExitStack

import concourse.bass as bass
from concourse import mybir

F32 = mybir.dt.float32
F32R = mybir.dt.float32r
I32 = mybir.dt.int32
U32 = mybir.dt.uint32
ALU = mybir.AluOpType
ACT = mybir.ActivationFunctionType
AX_X = mybir.AxisListType.X

P = 128
BATCH, CTX = 16, 512
PATCHES = (8, 16, 32)
N_SCALE = tuple((CTX - p) // (p // 2) + 1 for p in PATCHES)
N_AT = (0, N_SCALE[0], N_SCALE[0] + N_SCALE[1])
N = sum(N_SCALE)
N0, N1 = P, N - P
NE = N + 1
TAPS = sum(PATCHES)
TAP_AT = (0, PATCHES[0], PATCHES[0] + PATCHES[1])
R4 = 4
GROUP = 4
HEADS, DH = 8, 16
HALF = HEADS // 2
EPS = 1e-5
T_FFN, TOP_K, EXPERTS, FFN = 1024, 2, 8, 512
TJ = T_FFN // P
COLS = TJ * TOP_K
FC = FFN // P
N_TILES = T_FFN * TOP_K // P + EXPERTS - 1
TILE_N = (N0, N1)
RING = 4
ROUNDS = (N_TILES - 3) // RING
assert ROUNDS * RING + 3 == N_TILES
G_PREP, G_LAST = BATCH // GROUP - 2, BATCH // GROUP - 1
FFN_BATCHES = -(-T_FFN // N)
WT_PARTS = ((0, 8), (8, 24), (24, 40), (40, 56))

C_IDENT, C_TRI, C_ONES, C_IOTA, C_THR, C_LT, C_TILE = 0, P, 2 * P, 3 * P, 4 * P, 5 * P, 5 * P + 64
C_KONE = C_TILE + N_TILES * EXPERTS
C_SEL = C_KONE + 1
C_END = C_SEL + 16 * P
MAX_ROW = 48


def build(nc, x, wt, pos, bias, wqkv, wagg, bagg, consts, ew, ei, w1, w2, out):
    with ExitStack() as ctx:
        def sb(name, shape, dt=F32):
            return ctx.enter_context(nc.sbuf_tensor(name, shape, dt))

        def sem(name):
            return ctx.enter_context(nc.semaphore(name))

        x_sb = sb("x_sb", [P, BATCH, R4, CTX // R4])
        wt_sb = sb("wt_sb", [P, TAPS, P])
        pos_sb = sb("pos_sb", [P, N])
        bias_sb = sb("bias_sb", [P, 6])
        comb = sb("comb", [P, N])
        wqkv_sb = sb("wqkv_sb", [P, 3 * P])
        wagg_sb = sb("wagg_sb", [P, P])
        bagg_sb = sb("bagg_sb", [P, P])
        c_sb = sb("c_sb", [P, C_END])
        sel_r = sb("sel_r", [P, 4, 4, P], F32R)
        ident_r = sb("ident_r", [P, P], F32R)
        hT = sb("hT", [P, GROUP, N])
        h_sb = sb("h_sb", [P, 2, P])
        hb = sb("hb", [P, 2, 2, P])
        stats = sb("stats", [P, 2, 6])
        counts = sb("counts", [P, 2])
        mv = sb("mv", [P, 2, 2])
        var_eps = sb("var_eps", [P, 2])
        rstd = sb("rstd", [P, 2])
        eps_t = sb("eps_t", [P, TJ])
        mhalf_t = sb("mhalf_t", [P, TJ])
        z_sb = sb("z_sb", [P, 2, P])
        zT = sb("zT", [P, N])
        qk_hi = sb("qk_hi", [P, 2, NE], F32R)
        qk_lo = sb("qk_lo", [P, 2, NE], F32R)
        v_aug = sb("v_aug", [P, 2, 2, HEADS, 32])
        q_st = sb("q_st", [P, HALF, NE], F32R)
        k_st = sb("k_st", [P, HALF, NE], F32R)
        nmax = sb("nmax", [P, 2, HALF, P], F32R)
        probs = sb("probs", [P, 2, 2, 2, 2, NE])
        o_raw = sb("o_raw", [P, 2, N])
        rden = sb("rden", [P, 2, HEADS])
        o_sb = sb("o_sb", [P, 2, P])
        o_T = sb("o_T", [P, N])
        h1 = sb("h1", [P, 2, 2, P])
        w1_sb = sb("w1_sb", [P, EXPERTS, FFN])
        w2_sb = sb("w2_sb", [P, EXPERTS, FC, P])
        ew_sb = sb("ew_sb", [P, TJ, TOP_K])
        ei_sb = sb("ei_sb", [P, TJ, TOP_K], I32)
        ei_f = sb("ei_f", [P, COLS])
        onehot = sb("onehot", [P, COLS, EXPERTS])
        before = sb("before", [P, COLS + 1, EXPERTS])
        rank = sb("rank", [P, COLS, EXPERTS])
        cmp_t = sb("cmp_t", [P, EXPERTS, 16])
        tiles_e = sb("tiles_e", [P, EXPERTS])
        lt_t = sb("lt_t", [P, EXPERTS, EXPERTS])
        base_e = sb("base_e", [P, EXPERTS])
        end_e = sb("end_e", [P, EXPERTS])
        base_s = sb("base_s", [P, EXPERTS])
        slot_f = sb("slot_f", [P, COLS])
        slot_u = sb("slot_u", [P, COLS], U32)
        te_t = sb("te_t", [P, N_TILES, EXPERTS])
        te_f = sb("te_f", [P, N_TILES])
        te_i = sb("te_i", [P, N_TILES], I32)
        zero = sb("zero", [P, P])
        h1m = sb("h1m", [P, TJ, P])
        stats2 = sb("stats2", [P, TJ, 6])
        mv2 = sb("mv2", [P, TJ, 2])
        var_eps2 = sb("var_eps2", [P, TJ])
        rstd2 = sb("rstd2", [P, TJ])
        z2 = sb("z2", [P, TJ, P])
        zs = sb("zs", [P, RING, P])
        zsT = sb("zsT", [P, 2, P])
        w1_now = sb("w1_now", [P, 2, FFN])
        hidT = sb("hidT", [P, 2, FC, P])
        y_sb = sb("y_sb", [P, RING, P])
        g_sb = sb("g_sb", [P, COLS, P])

        tok_ps = ctx.enter_context(nc.psum_tensor("tok_ps", [P, 2, 512], F32))
        s_ps = ctx.enter_context(nc.psum_tensor("s_ps", [P, 4, 512], F32))
        m_ps = ctx.enter_context(nc.psum_tensor("m_ps", [P, 2, 512], F32))

        z_dram = nc.dram_tensor("z_slots", (N_TILES * P, P), F32, kind="Internal").ap()
        y_dram = nc.dram_tensor("y_slots", (N_TILES * P, P), F32, kind="Internal").ap()

        ident = c_sb[:, C_IDENT:C_IDENT + P]
        out_rows = out.rearrange("b n d -> (b n) d")

        consts_in, sel_in, small_in = sem("consts_in"), sem("sel_in"), sem("small_in")
        idx_in, ew_in = sem("idx_in"), sem("ew_in")
        x_in = [sem(f"x_in{g}") for g in range(BATCH // GROUP)]
        wt_in = [sem(f"wt_in{s}") for s in range(len(WT_PARTS))]
        w1_in, w2_in = sem("w1_in"), sem("w2_in")
        zero_set, z_cleared = sem("zero_set"), sem("z_cleared")
        pads_set, psum_set = sem("pads_set"), sem("psum_set")
        consts_r = sem("consts_r")
        comb_step, comb_ready = sem("comb_step"), sem("comb_ready")
        tok_done, hT_ready = sem("tok_done"), sem("hT_ready")
        h_turned, h_ready = sem("h_turned"), sem("h_ready")
        stats_ready, mv_ready = sem("stats_ready"), sem("mv_ready")
        eps_added, rstd_ready, hb_ready = sem("eps_added"), sem("rstd_ready"), sem("hb_ready")
        z_ready, z_turned, zT_ready = sem("z_ready"), sem("z_turned"), sem("zT_ready")
        qk_done, v_done = sem("qk_done"), sem("v_done")
        hi_ready, lo_ready, v_ready = sem("hi_ready"), sem("lo_ready"), sem("v_ready")
        stacked, q_st_ready, k_st_ready = sem("stacked"), sem("q_st_ready"), sem("k_st_ready")
        s1_done, max_ready = sem("s1_done"), sem("max_ready")
        max_placed, q_shifted = sem("max_placed"), sem("q_shifted")
        s2_done, probs_ready = sem("s2_done"), sem("probs_ready")
        pv_done, o_raw_ready, o_turned = sem("pv_done"), sem("o_raw_ready"), sem("o_turned")
        rden_ready, o_ready, on_turned, oT_ready = (
            sem("rden_ready"), sem("o_ready"), sem("on_turned"), sem("oT_ready"))
        agg_done, h1_ready = sem("agg_done"), sem("h1_ready")
        stored, h1_free = sem("stored"), sem("h1_free")
        route = sem("route")
        onehot_ready, counted = sem("onehot_ready"), sem("counted")
        routed = sem("routed")
        h1m_in, stats2_ready, mv2_ready = sem("h1m_in"), sem("stats2_ready"), sem("mv2_ready")
        eps2_added, rstd2_ready, z2_ready = sem("eps2_added"), sem("rstd2_ready"), sem("z2_ready")
        scattered = sem("scattered")
        zs_in = [sem(f"zs_in{i}") for i in range(RING)]
        zs_turned, zsT_ready = sem("zs_turned"), sem("zsT_ready")
        w1_ready, hid_done, hidT_ready = sem("w1_ready"), sem("hid_done"), sem("hidT_ready")
        y_done, y_ready = sem("y_done"), sem("y_ready")
        y_out = [sem(f"y_out{i}") for i in range(RING)]
        gathered = [sem(f"gathered{i}") for i in range(COLS // 4)]
        combined = sem("combined")
        final_out = sem("final_out")

        block = ctx.enter_context(nc.Block())

        @block.sync
        def _(sp):
            def load_x(g):
                gs = slice(GROUP * g, GROUP * (g + 1))
                sp.dma_start(x_sb[:, gs], x[:, gs]).then_inc(x_in[g], 16)

            def load_wt(n):
                lo, hi = WT_PARTS[n]
                sp.dma_start(wt_sb[:, lo:hi], wt[:, lo:hi]).then_inc(wt_in[n], 16)

            load_wt(0)
            load_x(0)
            load_wt(1)
            load_wt(2)
            load_wt(3)
            load_x(1)
            load_x(2)
            load_x(3)
            sp.dma_start(w1_sb[:], w1.rearrange("e h f -> h e f")).then_inc(w1_in, 16)
            sp.dma_start(w2_sb[:], w2.rearrange("e (c p) d -> p e c d", p=P)).then_inc(w2_in, 16)
            sp.wait_ge(zero_set, 1)
            sp.dma_start(z_dram.rearrange("(i p) d -> p i d", p=P),
                         zero[:].unsqueeze(1).to_broadcast([P, N_TILES, P])).then_inc(z_cleared, 16)

            def store_h1(b, par):
                to = out[b] if isinstance(b, int) else out[bass.ds(b, 1)].squeeze(0)
                sp.wait_ge(h1_ready, b + 1)
                sp.dma_start(to[0:N0, :], h1[:, par, 0, :]).then_inc(stored, 16)
                sp.dma_start(to[N0:N, :], h1[0:N1, par, 1, :]).then_inc(stored, 16)
                sp.wait_ge(stored, b * 32 + 32)
                sp.sem_inc(h1_free, 1)

            with sp.Fori(0, G_PREP * GROUP // 2) as i:
                for par in range(2):
                    store_h1(i * 2 + par, par)

            sp.wait_ge(stored, 32 * FFN_BATCHES)
            sp.dma_start(h1m[:], out_rows[0:T_FFN].rearrange("(j p) d -> p j d", p=P)).then_inc(h1m_in, 16)

            def load_zs(i, slot):
                sp.dma_start(zs[:, slot, :], z_dram[bass.ds(i * P, P), :]).then_inc(zs_in[slot], 16)

            def store_y(i, slot):
                sp.wait_ge(y_ready, i + 1)
                sp.dma_start(y_dram[bass.ds(i * P, P), :], y_sb[:, slot, :]).then_inc(y_out[slot], 16)

            for b in range(G_PREP * GROUP, G_LAST * GROUP - 1):
                store_h1(b, b % 2)
            sp.wait_ge(scattered, 16 * COLS)
            for i in range(RING):
                load_zs(i, i)
            store_h1(G_LAST * GROUP - 1, 1)
            with sp.Fori(0, ROUNDS - 1) as k:
                for slot in range(RING):
                    sp.wait_ge(zs_turned, k * RING + (slot + 1))
                    load_zs(k * RING + (slot + RING), slot)
                    store_y(k * RING + slot, slot)
            for i in range((ROUNDS - 1) * RING, N_TILES):
                if i + RING < N_TILES:
                    sp.wait_ge(zs_turned, i + 1)
                    load_zs(i + RING, i % RING)
                store_y(i, i % RING)
            for b in range(G_LAST * GROUP, BATCH):
                store_h1(b, b % 2)
            sp.wait_ge(combined, COLS)
            sp.dma_start(out_rows[0:T_FFN].rearrange("(j p) d -> p j d", p=P), h1m[:]).then_inc(final_out, 16)
            sp.wait_ge(final_out, 16)

        @block.gpsimd
        def _(pool):
            g = nc.gpsimd
            g.memset(zero[:], 0.0).then_inc(zero_set, 1)
            pool.sem_inc(h1_free, 2)
            g.memset(eps_t[:], EPS)
            g.memset(mhalf_t[:], -0.5)
            g.memset(qk_hi[:, :, N:NE].bitcast(F32), 0.0)
            g.memset(qk_lo[:, :, N:NE].bitcast(F32), 0.0)
            g.memset(nmax[:].bitcast(F32), 0.0)
            g.memset(v_aug[:], 0.0).then_inc(pads_set, 1)
            pool.wait_ge(pads_set, 1)
            g.memset(v_aug[:, :, :, :, DH:DH + 1], 1.0).then_inc(pads_set, 1)

            def stage1(b, par):
                pool.wait_ge(mv_ready, b * 2 + 2)
                g.tensor_tensor(var_eps[:], mv[:, :, 1], eps_t[:, 0:2], ALU.add).then_inc(eps_added, 1)
                pool.wait_ge(eps_added, b + 1)
                g.tensor_tensor(rstd[:], var_eps[:], mhalf_t[:, 0:2], ALU.pow).then_inc(rstd_ready, 1)
                pool.wait_ge(h_ready, b + 1)
                g.tensor_tensor(hb[:, par], h_sb[:], bagg_sb[:].unsqueeze(1).to_broadcast([P, 2, P]),
                                ALU.add).then_inc(hb_ready, 1)

            pool.wait_ge(small_in, 16 * 5)
            with pool.Fori(0, G_PREP * GROUP // 2) as i:
                for par in range(2):
                    stage1(i * 2 + par, par)

            def scatter(c):
                pool.wait_ge(z2_ready, c // TOP_K + 1)
                g.indirect_dma_start(
                    z_dram, bass.IndirectOffsetOnAxis(ap=slot_u[:, c:c + 1], axis=0),
                    z2[:, c // TOP_K, :], None).then_inc(scattered, 16)

            def gather(c):
                g.indirect_dma_start(
                    g_sb[:, c, :], None, y_dram,
                    bass.IndirectOffsetOnAxis(ap=slot_u[:, c:c + 1], axis=0)).then_inc(gathered[c // 4], 16)

            for b in range(G_PREP * GROUP, BATCH):
                stage1(b, b % 2)
                if b == G_PREP * GROUP + 1:
                    pool.wait_ge(mv2_ready, TJ)
                    g.tensor_tensor(var_eps2[:], mv2[:, :, 1], eps_t[:], ALU.add).then_inc(eps2_added, 1)
                    pool.wait_ge(eps2_added, 1)
                    g.tensor_tensor(rstd2[:], var_eps2[:], mhalf_t[:], ALU.pow).then_inc(rstd2_ready, 1)
                    pool.wait_ge(routed, 1)
                    pool.wait_ge(z_cleared, 16)
                if b in (G_PREP * GROUP + 2, G_PREP * GROUP + 3):
                    for c in range(COLS // 2):
                        scatter(c + COLS // 2 * (b % 2))
                if b == G_LAST * GROUP + 1:
                    for slot in range(RING):
                        pool.wait_ge(y_out[slot], 16 * len(range(slot, N_TILES, RING)))
                if b in (G_LAST * GROUP + 1, G_LAST * GROUP + 2):
                    for c in range(COLS // 2):
                        gather(c + COLS // 2 * ((b + 1) % 2))

        @block.scalar
        def _(act):
            s = nc.scalar

            def stage1_head(b, first=False):
                if not first:
                    act.wait_ge(hb_ready, b)
                act.wait_ge(h_turned, b + 1)
                s.copy(h_sb[:], m_ps[:, 0, 0:2 * P].rearrange("p (t d) -> p t d", t=2)).then_inc(h_ready, 1)

            def stage1_zT(b):
                act.wait_ge(z_turned, b + 1)
                s.copy(zT[:], m_ps[:, 1, 0:N]).then_inc(zT_ready, 1)

            def stage1_hi(b):
                act.wait_ge(qk_done, b + 1)
                s.copy(qk_hi[:, :, 0:N], m_ps[:, 0, 0:2 * N].rearrange("p (w n) -> p w n", w=2)).then_inc(hi_ready, 1)

            def stage1_v(b, par):
                act.wait_ge(v_done, b + 1)
                s.copy(v_aug[:, par, :, :, 0:DH],
                       m_ps[:, 1, 0:2 * P].rearrange("p (t h d) -> p t h d", t=2, h=HEADS)).then_inc(v_ready, 1)

            def stage1_k(b):
                for f in range(2):
                    act.wait_ge(stacked, b * 2 + (f + 1))
                    s.activation(k_st[:, 2 * f:2 * f + 2, :].rearrange("p j n -> p (j n)"),
                                 s_ps[:, 2 * f + 1, 0:2 * NE], ACT.Identity,
                                 bias=c_sb[:, C_KONE:C_KONE + 1]).then_inc(k_st_ready, 1)

            def exps(b, t, f):
                n = TILE_N[t]
                act.wait_ge(s2_done, b * 4 + (2 * t + f + 1))
                s.activation(probs[0:n, t, f].rearrange("p r j n -> p r (j n)"),
                             s_ps[0:n, 2 * f:2 * f + 2, 0:2 * NE], ACT.Exp,
                             scale=DH ** -0.5).then_inc(probs_ready, 1)

            def stage2_oraw(b):
                act.wait_ge(pv_done, b + 1)
                s.copy(o_raw[:], m_ps[:, 0, 0:2 * N].rearrange("p (r n) -> p r n", r=2)).then_inc(o_raw_ready, 1)

            def stage2_oT(b):
                act.wait_ge(on_turned, b + 1)
                s.copy(o_T[:], m_ps[:, 0, 0:N]).then_inc(oT_ready, 1)

            def slot(b, par):
                stage1_head(b + 1)
                exps(b, 0, 0)
                stage1_zT(b + 1)
                exps(b, 0, 1)
                stage1_hi(b + 1)
                exps(b, 1, 0)
                exps(b, 1, 1)
                stage1_k(b + 1)
                stage1_v(b + 1, 1 - par)
                stage2_oraw(b)
                stage2_oT(b)

            def gelu(i, par):
                act.wait_ge(hid_done, i + 1)
                s.activation(hidT[:, par].rearrange("p c s -> p (c s)"), s_ps[:, par, :],
                             ACT.Gelu).then_inc(hidT_ready, 1)

            act.dma_start(ei_sb[:], ei.rearrange("(j p) k -> p j k", p=P)).then_inc(idx_in, 16)
            act.dma_start(c_sb[:, 0:C_SEL], consts[:, 0:C_SEL]).then_inc(consts_in, 16)
            for dst, src in ((pos_sb, pos), (bias_sb, bias), (wqkv_sb, wqkv), (wagg_sb, wagg), (bagg_sb, bagg)):
                act.dma_start(dst[:], src).then_inc(small_in, 16)
            act.dma_start(c_sb[:, C_SEL:C_END], consts[:, C_SEL:C_END]).then_inc(sel_in, 16)
            act.dma_start(ew_sb[:], ew.rearrange("(j p) k -> p j k", p=P)).then_inc(ew_in, 16)
            act.wait_ge(pads_set, 2)
            act.wait_ge(consts_in, 16)
            stage1_head(0, True)
            stage1_zT(0)
            stage1_hi(0)
            stage1_k(0)
            stage1_v(0, 0)
            with act.Fori(0, G_PREP) as g:
                for j in range(GROUP):
                    slot(g * GROUP + j, j % 2)
            for j in range(GROUP):
                slot(G_PREP * GROUP + j, j % 2)
            for i in range(RING):
                gelu(i, i % 2)
            with act.Fori(1, ROUNDS) as k:
                for i in range(RING):
                    gelu(k * RING + i, i % 2)
            for i in range(ROUNDS * RING, N_TILES):
                gelu(i, i % 2)
            for j in range(GROUP - 1):
                slot(G_LAST * GROUP + j, j % 2)
            for t in range(2):
                for f in range(2):
                    exps(BATCH - 1, t, f)
            stage2_oraw(BATCH - 1)
            stage2_oT(BATCH - 1)

        @block.vector
        def _(dve):
            v = nc.vector
            v.memset(m_ps[:], 0.0).then_inc(psum_set, 1)
            dve.wait_ge(consts_in, 16)
            v.tensor_copy(ident_r[:], ident).then_inc(consts_r, 1)
            steps = [0]

            def link(ins):
                steps[0] += 1
                ins.then_inc(route, 1)
                dve.wait_ge(route, steps[0])

            dve.wait_ge(idx_in, 16)
            link(v.tensor_copy(ei_f[:], ei_sb[:].rearrange("p j k -> p (j k)")))
            v.tensor_tensor(onehot[:], ei_f[:].unsqueeze(2).to_broadcast([P, COLS, EXPERTS]),
                            c_sb[:, C_IOTA:C_IOTA + P].rearrange("p (c e) -> p c e", e=EXPERTS),
                            ALU.is_equal).then_inc(onehot_ready, 1)
            link(v.memset(before[:, 0, :], 0.0))
            dve.wait_ge(counted, 2)
            for c in range(COLS):
                link(v.tensor_tensor(before[:, c + 1, :], before[:, c, :],
                                     s_ps[:, 1, c * EXPERTS:(c + 1) * EXPERTS], ALU.add))
            total = before[:, COLS, :]
            link(v.tensor_tensor(cmp_t[:], total.unsqueeze(2).to_broadcast([P, EXPERTS, 16]),
                                 c_sb[:, C_THR:C_THR + P].rearrange("p (e m) -> p e m", m=16), ALU.is_gt))
            link(v.tensor_reduce(tiles_e[:], cmp_t[:], AX_X, ALU.add))
            link(v.tensor_tensor(lt_t[:], tiles_e[:].unsqueeze(1).to_broadcast([P, EXPERTS, EXPERTS]),
                                 c_sb[:, C_LT:C_LT + 64].rearrange("p (e f) -> p e f", f=EXPERTS), ALU.mult))
            link(v.tensor_reduce(base_e[:], lt_t[:], AX_X, ALU.add))
            link(v.tensor_tensor(end_e[:], base_e[:], tiles_e[:], ALU.add))
            link(v.tensor_scalar(base_s[:], base_e[:], float(P), None, ALU.mult))
            link(v.tensor_tensor(rank[:], before[:, 0:COLS, :],
                                 s_ps[:, 0, 0:P].rearrange("p (c e) -> p c e", e=EXPERTS), ALU.add))
            link(v.tensor_tensor(rank[:], rank[:], base_s[:].unsqueeze(1).to_broadcast([P, COLS, EXPERTS]), ALU.add))
            link(v.tensor_tensor(rank[:], rank[:], onehot[:], ALU.mult))
            link(v.tensor_reduce(slot_f[:], rank[:], AX_X, ALU.add))
            link(v.tensor_copy(slot_u[:], slot_f[:]))
            link(v.tensor_tensor(te_t[:], end_e[:].unsqueeze(1).to_broadcast([P, N_TILES, EXPERTS]),
                                 c_sb[:, C_TILE:C_TILE + N_TILES * EXPERTS].rearrange("p (i e) -> p i e", e=EXPERTS),
                                 ALU.is_le))
            link(v.tensor_reduce(te_f[:], te_t[:], AX_X, ALU.add))
            v.tensor_scalar(te_i[:], te_f[:], float(EXPERTS - 1), None, ALU.min).then_inc(routed, 1)

            dve.wait_ge(sel_in, 16)
            v.tensor_copy(sel_r[:].rearrange("p a j m -> p (a j m)"),
                          c_sb[:, C_SEL:C_SEL + 16 * P]).then_inc(consts_r, 1)
            dve.wait_ge(small_in, 16 * 5)
            for i in range(3):
                v.tensor_scalar(comb[:, N_AT[i]:N_AT[i] + N_SCALE[i]], pos_sb[:, N_AT[i]:N_AT[i] + N_SCALE[i]],
                                bias_sb[:, i:i + 1], bias_sb[:, 3 + i:4 + i], ALU.add, ALU.add).then_inc(comb_ready, 1)
            dve.wait_ge(comb_ready, 3)

            def hT_evac(g):
                dve.wait_ge(tok_done, g * 3 + 3)
                for i, src in enumerate((tok_ps[:, 0, 0:GROUP * N_SCALE[0]],
                                         tok_ps[:, 1, 0:GROUP * N_SCALE[1]],
                                         tok_ps[:, 1, GROUP * N_SCALE[1]:GROUP * (N_SCALE[1] + N_SCALE[2])])):
                    a, n = N_AT[i], N_SCALE[i]
                    v.tensor_tensor(hT[:, :, a:a + n], src.rearrange("p (b n) -> p b n", b=GROUP),
                                    comb[:, a:a + n].unsqueeze(1).to_broadcast([P, GROUP, n]),
                                    ALU.add).then_inc(hT_ready, 1)

            def stage1_stats(b):
                dve.wait_ge(h_ready, b + 1)
                for t in range(2):
                    v.bn_stats(stats[:, t, :], h_sb[:, t, :]).then_inc(stats_ready, 1)
                dve.wait_ge(stats_ready, b * 2 + 2)
                v.tensor_copy(counts[:], stats[:, :, 0])
                for t in range(2):
                    v.bn_aggr(mv[:, t, :], stats[:, t, :]).then_inc(mv_ready, 1)

            def stage1_z(b):
                dve.wait_ge(rstd_ready, b + 1)
                for t in range(2):
                    v.tensor_scalar(z_sb[:, t, :], h_sb[:, t, :], mv[:, t, 0:1], rstd[:, t:t + 1],
                                    ALU.subtract, ALU.mult).then_inc(z_ready, 1)

            def stage1_lo(b):
                dve.wait_ge(hi_ready, b + 1)
                v.tensor_tensor(qk_lo[:, :, 0:N], m_ps[:, 0, 0:2 * N].rearrange("p (w n) -> p w n", w=2),
                                qk_hi[:, :, 0:N].bitcast(F32), ALU.subtract).then_inc(lo_ready, 1)

            def stage1_max(b, t):
                n = TILE_N[t]
                for f in range(2):
                    dve.wait_ge(s1_done, b * 4 + (2 * t + f + 1))
                    dst = nmax[0:n, t, 2 * f:2 * f + 2, :].rearrange("p j (r m) -> p r j m", r=2)[:, :, :, MAX_ROW]
                    src = s_ps[0:n, 2 * f:2 * f + 2, 0:2 * NE].rearrange("p r (j n) -> p r j n", j=2)[:, :, :, 0:N]
                    v.tensor_reduce(dst, src, AX_X, ALU.max, negate=True).then_inc(max_ready, 1)

            def stage1_q(b):
                for f in range(2):
                    dve.wait_ge(stacked, b * 2 + (f + 1))
                    v.tensor_copy(q_st[:, 2 * f:2 * f + 2, :].rearrange("p j n -> p (j n)"),
                                  s_ps[:, 2 * f, 0:2 * NE]).then_inc(q_st_ready, 1)

            def stage2_shift(b):
                for f in range(2):
                    dve.wait_ge(max_placed, b * 2 + (f + 1))
                    qv = q_st[:, 2 * f:2 * f + 2, :].rearrange("p j n -> p (j n)")
                    v.tensor_tensor(qv, s_ps[:, 2 * f, 0:2 * NE], qv.bitcast(F32), ALU.add).then_inc(q_shifted, 1)

            def stage2_norm(b):
                dve.wait_ge(o_turned, b + 1)
                for t in range(2):
                    n = TILE_N[t]
                    o = m_ps[0:n, 1, 256 * t:256 * (t + 1)].rearrange("p (h e) -> p h e", e=32)
                    v.reciprocal(rden[0:n, t, :], o[:, :, DH]).then_inc(rden_ready, 1)
                dve.wait_ge(rden_ready, b * 2 + 2)
                for t in range(2):
                    n = TILE_N[t]
                    o = m_ps[0:n, 1, 256 * t:256 * (t + 1)].rearrange("p (h e) -> p h e", e=32)
                    v.tensor_tensor(o_sb[0:n, t, :].rearrange("p (h d) -> p h d", d=DH), o[:, :, 0:DH],
                                    rden[0:n, t, :].unsqueeze(2).to_broadcast([n, HEADS, DH]),
                                    ALU.mult).then_inc(o_ready, 1)

            def stage2_h1(b, par):
                dve.wait_ge(agg_done, b + 1)
                dve.wait_ge(hb_ready, b + 1)
                dve.wait_ge(h1_free, b + 1)
                v.tensor_tensor(h1[:, par], m_ps[:, 1, 0:2 * P].rearrange("p (t d) -> p t d", t=2),
                                hb[:, par], ALU.add).then_inc(h1_ready, 1)

            def slot(b, par, j, g=None, extra=None):
                stage1_stats(b + 1)
                stage2_shift(b)
                stage1_z(b + 1)
                stage1_lo(b + 1)
                stage1_q(b + 1)
                stage1_max(b + 1, 0)
                stage2_norm(b)
                stage1_max(b + 1, 1)
                if extra is not None:
                    extra(j)
                if j == GROUP - 2 and g is not None:
                    hT_evac(g + 1)
                stage2_h1(b, par)

            def prepare(j):
                if j == 0:
                    dve.wait_ge(h1m_in, 16)
                    for i in range(TJ):
                        v.bn_stats(stats2[:, i, :], h1m[:, i, :]).then_inc(stats2_ready, 1)
                    for i in range(TJ):
                        dve.wait_ge(stats2_ready, i + 1)
                        v.bn_aggr(mv2[:, i, :], stats2[:, i, :]).then_inc(mv2_ready, 1)
                if j == 1:
                    dve.wait_ge(rstd2_ready, 1)
                    for i in range(TJ):
                        v.tensor_scalar(z2[:, i, :], h1m[:, i, :], mv2[:, i, 0:1], rstd2[:, i:i + 1],
                                        ALU.subtract, ALU.mult).then_inc(z2_ready, 1)

            def combine(cols):
                for c in cols:
                    i, k = c // TOP_K, c % TOP_K
                    dve.wait_ge(gathered[c // 4], 64)
                    dve.wait_ge(ew_in, 16)
                    if k:
                        dve.wait_ge(combined, c)
                    v.scalar_tensor_tensor(out=h1m[:, i, :], in0=g_sb[:, c, :], scalar=ew_sb[:, i, k:k + 1],
                                           in1=h1m[:, i, :], op0=ALU.mult, op1=ALU.add).then_inc(combined, 1)

            def zsT_evac(i, par):
                dve.wait_ge(zs_turned, i + 1)
                v.tensor_copy(zsT[:, par, :], m_ps[:, 0, 0:P]).then_inc(zsT_ready, 1)

            def fetch_w1(i, par, first=False):
                e = dve.value_load(te_i[0:1, bass.ds(i, 1)], min_val=0, max_val=EXPERTS - 1)
                if not first:
                    dve.wait_ge(hid_done, i - 1)
                v.tensor_copy(w1_now[:, par, :],
                              w1_sb[:, bass.ds(e, 1), :].rearrange("p a f -> p (a f)")).then_inc(w1_ready, 1)

            def y_evac(i, slot, rounds=None):
                dve.wait_ge(y_done, i + 1)
                if rounds is not None:
                    dve.wait_ge(y_out[slot], rounds * 16)
                v.tensor_copy(y_sb[:, slot, :], m_ps[:, 1, 0:P]).then_inc(y_ready, 1)

            def step(i, slot, more_z, more_w, rounds):
                par = slot % 2
                if more_z:
                    zsT_evac(i + 2, par)
                if more_w:
                    fetch_w1(i + 3, 1 - par)
                y_evac(i, slot, rounds)

            hT_evac(0)
            stage1_stats(0)
            stage1_z(0)
            stage1_lo(0)
            stage1_q(0)
            stage1_max(0, 0)
            stage1_max(0, 1)
            with dve.Fori(0, G_PREP) as g:
                for j in range(GROUP):
                    slot(g * GROUP + j, j % 2, j, g)
            for j in range(GROUP):
                slot(G_PREP * GROUP + j, j % 2, j, G_PREP, prepare)
            dve.wait_ge(w1_in, 16)
            fetch_w1(0, 0, True)
            fetch_w1(1, 1, True)
            zsT_evac(0, 0)
            zsT_evac(1, 1)
            fetch_w1(2, 0)
            for i in range(RING):
                step(i, i, True, True, None)
            with dve.Fori(1, ROUNDS) as k:
                for i in range(RING):
                    step(k * RING + i, i, True, True, k)
            for i in range(ROUNDS * RING, N_TILES):
                step(i, i % RING, i + 2 < N_TILES, i + 3 < N_TILES, i // RING)
            for j in range(GROUP - 1):
                slot(G_LAST * GROUP + j, j % 2, j)
            stage2_shift(BATCH - 1)
            combine(range(0, COLS // 2))
            stage2_norm(BATCH - 1)
            combine(range(COLS // 2, COLS))
            stage2_h1(BATCH - 1, 1)

        @block.tensor
        def _(pe):
            def tok(g, lo, hi):
                for c in range(lo, hi):
                    i = 0 if c < TAP_AT[1] else 1 if c < TAP_AT[2] else 2
                    t = c - TAP_AT[i]
                    st = PATCHES[i] // 2 // R4
                    q0, n = t // R4, N_SCALE[i]
                    xs = x_sb[:, bass.ds(g * GROUP, GROUP), t % R4, q0:q0 + (n - 1) * st + 1:st]
                    o0 = 0 if i < 2 else GROUP * N_SCALE[1]
                    dst = tok_ps[:, min(i, 1), o0:o0 + GROUP * n].rearrange("p (b n) -> p b n", b=GROUP)
                    mm = pe.matmul(dst, wt_sb[:, c, :], xs, start=(t == 0), stop=(t == PATCHES[i] - 1))
                    if t == PATCHES[i] - 1:
                        mm.then_inc(tok_done, 1)

            def h_turn(j):
                pe.transpose(m_ps[:, 0, 0:P], hT[:, j, 0:N0], ident)
                pe.transpose(m_ps[0:N1, 0, P:2 * P], hT[:, j, N0:N], ident).then_inc(h_turned, 1)

            def z_turn(b):
                pe.wait_ge(z_ready, b * 2 + 2)
                pe.transpose(m_ps[:, 1, 0:N0], z_sb[:, 0, :], ident)
                pe.transpose(m_ps[:, 1, N0:N], z_sb[0:N1, 1, :], ident[0:N1, 0:N1]).then_inc(z_turned, 1)

            def project(b):
                pe.wait_ge(zT_ready, b + 1)
                for w in range(2):
                    mm = pe.matmul(m_ps[:, 0, w * N:(w + 1) * N], wqkv_sb[:, w * P:(w + 1) * P], zT[:],
                                   start=True, stop=True)
                mm.then_inc(qk_done, 1)
                pe.matmul(m_ps[:, 1, 0:P], zT[:, 0:N0], wqkv_sb[:, 2 * P:3 * P], start=True, stop=True)
                pe.matmul(m_ps[0:N1, 1, P:2 * P], zT[:, N0:N], wqkv_sb[:, 2 * P:3 * P],
                          start=True, stop=True).then_inc(v_done, 1)

            def stack(b, first=False):
                pe.wait_ge(lo_ready, b + 1)
                for f in range(2):
                    if not first:
                        pe.wait_ge(probs_ready, b * 4 + (f - 1))
                    for w in range(2):
                        for jj in range(2):
                            j = 2 * f + jj
                            dst = s_ps[:, 2 * f + w, jj * NE:(jj + 1) * NE]
                            pe.matmul(dst, sel_r[:, 2 * w, j, :], qk_hi[:, w, :], start=True, stop=False)
                            mm = pe.matmul(dst, sel_r[:, 2 * w + 1, j, :], qk_lo[:, w, :], start=False, stop=True)
                    mm.then_inc(stacked, 1)

            def scores(a, bb, t, f, done):
                n = TILE_N[t]
                for jj in range(2):
                    for r in range(2):
                        j = 2 * f + jj
                        mm = pe.matmul(s_ps[0:n, 2 * f + r, jj * NE:(jj + 1) * NE],
                                       a[64 * r:64 * r + 64, j, P * t:P * t + n], bb[64 * r:64 * r + 64, j, :],
                                       start=True, stop=True)
                mm.then_inc(done, 1)

            def s1(b, t, f):
                if t == 0:
                    pe.wait_ge(q_st_ready, b * 2 + (f + 1))
                    pe.wait_ge(k_st_ready, b * 2 + (f + 1))
                else:
                    pe.wait_ge(max_ready, b * 4 + (f + 1))
                scores(q_st, k_st, t, f, s1_done)

            def place_max(b, f):
                pe.wait_ge(max_ready, b * 4 + (3 + f))
                for jj in range(2):
                    for t in range(2):
                        n = TILE_N[t]
                        w = P if t == 0 else NE - P
                        o = jj * NE + P * t
                        mm = pe.matmul(s_ps[:, 2 * f, o:o + w], nmax[0:n, t, 2 * f + jj, :], ident_r[0:n, 0:w],
                                       start=True, stop=True)
                mm.then_inc(max_placed, 1)

            def s2(b, t, f):
                if t == 0:
                    pe.wait_ge(q_shifted, b * 2 + (f + 1))
                else:
                    pe.wait_ge(probs_ready, b * 4 + (f + 1))
                scores(k_st, q_st, t, f, s2_done)

            def pv(b, par, r, last=False):
                if r == 0:
                    pe.wait_ge(probs_ready, b * 4 + 4)
                    if not last:
                        pe.wait_ge(lo_ready, b + 2)
                for t in range(2):
                    n = TILE_N[t]
                    for j in range(HALF):
                        mm = pe.matmul(m_ps[32 * j:32 * j + 32, 0, r * N:(r + 1) * N],
                                       v_aug[0:n, par, t, HALF * r + j, :],
                                       probs[0:n, t, j // 2, r, j % 2, 0:N],
                                       start=(t == 0), stop=(t == 1))
                if r == 1:
                    mm.then_inc(pv_done, 1)

            def o_turn(b):
                pe.wait_ge(o_raw_ready, b + 1)
                for t in range(2):
                    n = TILE_N[t]
                    for r in range(2):
                        mm = pe.transpose(m_ps[0:n, 1, 256 * t + P * r:256 * t + P * (r + 1)],
                                          o_raw[:, r, P * t:P * t + n], ident)
                mm.then_inc(o_turned, 1)

            def on_turn(b):
                pe.wait_ge(o_ready, b * 2 + 2)
                pe.transpose(m_ps[:, 0, 0:N0], o_sb[:, 0, :], ident)
                pe.transpose(m_ps[:, 0, N0:N], o_sb[0:N1, 1, :], ident[0:N1, 0:N1]).then_inc(on_turned, 1)

            def aggregate(b):
                pe.wait_ge(oT_ready, b + 1)
                pe.matmul(m_ps[:, 1, 0:P], o_T[:, 0:N0], wagg_sb[:], start=True, stop=True)
                pe.matmul(m_ps[0:N1, 1, P:2 * P], o_T[:, N0:N], wagg_sb[:], start=True,
                          stop=True).then_inc(agg_done, 1)

            def weight(c):
                return 4 if c < TAP_AT[1] else 2 if c < TAP_AT[2] else 1

            SHARE = (0, 5, 12, 28, TAPS)
            FILL = (4, 2, 2, 2, 2, 4, 2, 2, 2, 1)

            pe.wait_ge(x_in[0], 16)
            for n, (lo, hi) in enumerate(WT_PARTS):
                pe.wait_ge(wt_in[n], 16)
                tok(0, lo, hi)
                if n == 0:
                    pe.wait_ge(consts_in, 16)
                    pe.wait_ge(onehot_ready, 1)
                    oh = onehot[:].rearrange("p c e -> p (c e)")
                    for bank, c in enumerate((C_TRI, C_ONES)):
                        pe.matmul(s_ps[:, bank, 0:P], c_sb[:, c:c + P], oh, start=True,
                                  stop=True).then_inc(counted, 1)
            pe.wait_ge(psum_set, 1)
            pe.wait_ge(hT_ready, 3)
            h_turn(0)
            pe.wait_ge(x_in[1], 16)
            tok(1, SHARE[0], SHARE[1])
            z_turn(0)
            pe.wait_ge(small_in, 16 * 5)
            project(0)
            pe.wait_ge(consts_r, 2)
            pe.wait_ge(routed, 1)
            stack(0, first=True)
            for t in range(2):
                for f in range(2):
                    s1(0, t, f)
            for q in x_in[1:]:
                pe.wait_ge(q, 16)

            def slot(group, j, g=None):
                b, par = group * GROUP + j, j % 2
                share = (j + 1) % GROUP
                lo, hi = (SHARE[share], SHARE[share + 1]) if g is not None else (0, 0)
                whole = sum(weight(c) for c in range(lo, hi))
                at = [lo, 0]
                if share == 0:
                    pe.wait_ge(hT_ready, group * 3 + 6)

                def fill(n):
                    start = at[0]
                    while at[0] < hi and at[1] < sum(FILL[:n + 1]) * whole / sum(FILL):
                        at[1] += weight(at[0])
                        at[0] += 1
                    if at[0] > start:
                        tok(g, start, at[0])

                h_turn((j + 1) % GROUP)
                fill(0)
                place_max(b, 0)
                place_max(b, 1)
                fill(1)
                s2(b, 0, 0)
                s2(b, 0, 1)
                fill(2)
                z_turn(b + 1)
                fill(3)
                project(b + 1)
                s2(b, 1, 0)
                fill(4)
                s2(b, 1, 1)
                fill(5)
                stack(b + 1)
                pv(b, par, 0)
                s1(b + 1, 0, 0)
                pv(b, par, 1)
                s1(b + 1, 0, 1)
                fill(6)
                o_turn(b)
                fill(7)
                s1(b + 1, 1, 0)
                s1(b + 1, 1, 1)
                fill(8)
                on_turn(b)
                fill(9)
                aggregate(b)

            with pe.Fori(0, G_PREP) as g:
                for j in range(GROUP):
                    slot(g, j, g + (2 if j == GROUP - 1 else 1))
            for j in range(GROUP):
                slot(G_PREP, j, G_LAST if j < GROUP - 1 else None)

            def zs_turn(i, slot, loads):
                pe.wait_ge(zs_in[slot], loads * 16)
                pe.transpose(m_ps[:, 0, 0:P], zs[:, slot, :], ident).then_inc(zs_turned, 1)

            def hidden(i, par):
                pe.wait_ge(zsT_ready, i + 1)
                pe.wait_ge(w1_ready, i + 1)
                for c in range(FC):
                    mm = pe.matmul(s_ps[:, par, c * P:(c + 1) * P], w1_now[:, par, c * P:(c + 1) * P],
                                   zsT[:, par, :], start=True, stop=True)
                mm.then_inc(hid_done, 1)

            def down(i, par, prev):
                e = pe.value_load(te_i[0:1, bass.ds(i, 1)], min_val=0, max_val=EXPERTS - 1)
                if prev:
                    pe.wait_ge(y_ready, i)
                pe.wait_ge(hidT_ready, i + 1)
                for c in range(FC):
                    mm = pe.matmul(m_ps[:, 1, 0:P], hidT[:, par, c, :],
                                   w2_sb[:, bass.ds(e, 1), c, :].rearrange("p a d -> p (a d)"),
                                   start=(c == 0), stop=(c == FC - 1))
                mm.then_inc(y_done, 1)

            def step(i, slot, rounds, more_z, more_h, prev=True):
                par = slot % 2
                if more_h:
                    hidden(i + 1, 1 - par)
                if more_z:
                    zs_turn(i + 2, (slot + 2) % RING, rounds + (1 if slot < 2 else 2))
                down(i, par, prev)

            pe.wait_ge(w2_in, 16)
            zs_turn(0, 0, 1)
            pe.wait_ge(max_ready, 4 * (G_LAST * GROUP + 1))
            hidden(0, 0)
            zs_turn(1, 1, 1)
            pe.wait_ge(h1_ready, G_LAST * GROUP)
            step(0, 0, 0, True, True, False)
            for i in range(1, RING):
                step(i, i, 0, True, True)
            with pe.Fori(1, ROUNDS) as k:
                for i in range(RING):
                    step(k * RING + i, i, k, True, True)
            for i in range(ROUNDS * RING, N_TILES):
                step(i, i % RING, i // RING, i + 2 < N_TILES, i + 1 < N_TILES)

            for j in range(GROUP - 1):
                slot(G_LAST, j)
            b = BATCH - 1
            place_max(b, 0)
            place_max(b, 1)
            for t in range(2):
                for f in range(2):
                    s2(b, t, f)
            pv(b, 1, 0, last=True)
            pv(b, 1, 1, last=True)
            o_turn(b)
            on_turn(b)
            aggregate(b)


def constants(np):
    c = np.zeros((P, C_END), np.float32)
    c[:, C_IDENT:C_IDENT + P] = np.eye(P)
    sel = np.zeros((P, 4, HALF, P), np.float32)
    for r in range(2):
        for j in range(HALF):
            for d in range(DH):
                src = (HALF * r + j) * DH + d
                row = 64 * r + d
                for which, blocks in enumerate(((0, 1), (2,), (0, 2), (1,))):
                    for blk in blocks:
                        sel[src, which, j, row + DH * blk] = 1.0
    c[:, C_SEL:C_SEL + 16 * P] = sel.reshape(P, -1)
    c[:, C_TRI:C_TRI + P] = np.triu(np.ones((P, P)), 1)
    c[:, C_ONES:C_ONES + P] = 1.0
    c[:, C_IOTA:C_IOTA + P] = np.tile(np.arange(EXPERTS), COLS)
    c[:, C_THR:C_THR + P] = np.tile(np.arange(16) * P, EXPERTS)
    c[:, C_LT:C_LT + 64] = np.tril(np.ones((EXPERTS, EXPERTS)), -1).reshape(-1)
    c[:, C_TILE:C_TILE + N_TILES * EXPERTS] = np.repeat(np.arange(N_TILES), EXPERTS)
    c[MAX_ROW, C_KONE] = c[64 + MAX_ROW, C_KONE] = 1.0
    return c


def kernel(**inputs):
    import numpy as np
    import concourse.bacc as bacc
    from concourse.bass_utils import run_bass_kernel_spmd

    a = {k: np.asarray(v) for k, v in inputs.items()}
    arrays = {
        "x": a["x"].transpose(2, 0, 1).reshape(P, BATCH, CTX // R4, R4).transpose(0, 1, 3, 2),
        "wt": np.concatenate([a[f"L0_tok_W{i}"].reshape(P, p, P).transpose(2, 1, 0)
                              for i, p in enumerate(PATCHES)], axis=1),
        "pos": np.concatenate([a[f"L0_tok_pos{i}"][0] for i in range(3)], axis=0).T,
        "bias": np.stack([a[f"L0_tok_b{i}"] for i in range(3)]
                         + [a["L0_tok_scale_emb"][i] for i in range(3)], axis=1),
        "wqkv": a["L0_attn_w_qkv"].T,
        "wagg": a["L0_attn_w_agg"].T,
        "bagg": np.broadcast_to(a["L0_attn_b_agg"][None, :], (P, P)),
        "consts": constants(np),
        "ew": a["L0_ffn_expert_weights"],
        "ei": a["L0_ffn_expert_indices"],
        "w1": a["L0_ffn_w1"],
        "w2": a["L0_ffn_w2"],
    }
    arrays = {k: np.ascontiguousarray(v) for k, v in arrays.items()}
    nc = bacc.Bacc("TRN2", target_bir_lowering=False, num_devices=1)
    aps = [nc.dram_tensor(k, v.shape, mybir.dt.from_np(v.dtype), kind="ExternalInput").ap() for k, v in arrays.items()]
    out = nc.dram_tensor("out", (BATCH, N, P), F32, kind="ExternalOutput").ap()
    build(nc, *aps, out)
    r = run_bass_kernel_spmd(nc, [arrays], core_ids=[0])
    return r.results[0]["out"]
```

```python
from contextlib import ExitStack

import concourse.bass as bass
from concourse import mybir

F32 = mybir.dt.float32
F32R = mybir.dt.float32r
I32 = mybir.dt.int32
U32 = mybir.dt.uint32
ALU = mybir.AluOpType
ACT = mybir.ActivationFunctionType
AX_X = mybir.AxisListType.X

P = 128
BATCH, CTX = 16, 512
PATCHES = (8, 16, 32)
N_SCALE = tuple((CTX - p) // (p // 2) + 1 for p in PATCHES)
N_AT = (0, N_SCALE[0], N_SCALE[0] + N_SCALE[1])
N = sum(N_SCALE)
N0, N1 = P, N - P
NE = N + 1
TAPS = sum(PATCHES)
TAP_AT = (0, PATCHES[0], PATCHES[0] + PATCHES[1])
WIDE_TAPS = TAP_AT[2]
R4 = 4
GROUP = 4
HEADS, DH = 8, 16
HALF = HEADS // 2
EPS = 1e-5
T_FFN, TOP_K, EXPERTS, FFN = 1024, 2, 8, 512
TJ = T_FFN // P
COLS = TJ * TOP_K
FC = FFN // P
N_TILES = T_FFN * TOP_K // P + EXPERTS - 1
TILE_N = (N0, N1)
G_PREP, G_LAST = BATCH // GROUP - 2, BATCH // GROUP - 1
PART = 3
ROUND = 2 * PART
ROUNDS = -(-N_TILES // ROUND)
EXPERT_SLOT = G_PREP * GROUP + 2


def tiles_of(n, lo, hi):
    if n is None or not 0 <= n < ROUNDS:
        return range(0)
    return range(n * ROUND + lo, min(n * ROUND + hi, N_TILES))


def part_tiles(n, h):
    return tiles_of(n, h * PART, (h + 1) * PART)


FFN_BATCHES = -(-T_FFN // N)
FINAL_PARTS = ((0, TJ // 2), (TJ // 2, TJ))
H1M_AFTER = FFN_BATCHES + FFN_BATCHES % 2
WT_PARTS = ((0, 2), (2, 8), (8, 16), (16, 24), (24, 32), (32, 40), (40, 56))
TAP_ORDER = tuple(tuple(sorted(range(p), key=lambda t: (t % R4, t))) for p in PATCHES)

C_IDENT, C_TRI, C_ONES, C_IOTA, C_THR, C_LT, C_TILE = 0, P, 2 * P, 3 * P, 4 * P, 5 * P, 5 * P + 64
C_KONE = C_TILE + N_TILES * EXPERTS
C_SEL = C_KONE + HALF
C_END = C_SEL + 16 * P
MAX_ROW = 48


def build(nc, x, wt, pos, bias, wqkv, wagg, bagg, consts, ew, ei, w1, w2, out):
    with ExitStack() as ctx:
        def sb(name, shape, dt=F32):
            return ctx.enter_context(nc.sbuf_tensor(name, shape, dt))

        def sem(name):
            return ctx.enter_context(nc.semaphore(name))

        x_sb = sb("x_sb", [P, BATCH, R4, CTX // R4])
        wt_sb = sb("wt_sb", [P, TAPS, P])
        bias_sb = sb("bias_sb", [P, 6])
        comb = sb("comb", [P, N])
        wqkv_sb = sb("wqkv_sb", [P, 3 * P])
        wagg_sb = sb("wagg_sb", [P, P])
        bagg_sb = sb("bagg_sb", [P, P])
        c_sb = sb("c_sb", [P, C_SEL])
        sel_r = sb("sel_r", [P, 4, 4, P], F32R)
        ident_r = sb("ident_r", [P, P], F32R)
        hT = sb("hT", [P, GROUP, N])
        h_sb = sb("h_sb", [P, 2, P])
        hb = sb("hb", [P, 2, 2, P])
        stats = sb("stats", [P, 2, 6])
        counts = sb("counts", [P, 2])
        mv = sb("mv", [P, 2, 2])
        var_eps = sb("var_eps", [P, 2])
        rstd = sb("rstd", [P, 2])
        eps_t = sb("eps_t", [P, TJ])
        mhalf_t = sb("mhalf_t", [P, TJ])
        z_sb = sb("z_sb", [P, 2, P])
        zT = sb("zT", [P, N])
        qk_hi = sb("qk_hi", [P, 2, NE], F32R)
        qk_lo = sb("qk_lo", [P, 2, NE], F32R)
        v_aug = sb("v_aug", [P, 2, 2, HEADS, 32])
        q_st = sb("q_st", [P, HALF, NE], F32R)
        k_st = sb("k_st", [P, HALF, NE], F32R)
        nmax = sb("nmax", [P, 2, P], F32R)
        probs = sb("probs", [P, 2, 2, 2, 2, NE])
        o_raw = sb("o_raw", [P, 2, N])
        warm, mark = sb("warm", [P, 1]), sb("mark", [P, 1])
        rden = sb("rden", [P, 2, HEADS])
        o_sb = sb("o_sb", [P, 2, P])
        o_T = sb("o_T", [P, N])
        h1 = sb("h1", [P, 2, 2, P])
        w1_sb = sb("w1_sb", [P, EXPERTS, FFN])
        w2_sb = sb("w2_sb", [P, EXPERTS, FC, P])
        ew_sb = sb("ew_sb", [P, TJ, TOP_K])
        ei_sb = sb("ei_sb", [P, TJ, TOP_K], I32)
        ei_f = sb("ei_f", [P, COLS])
        onehot = sb("onehot", [P, COLS, EXPERTS])
        before = sb("before", [P, COLS + 1, EXPERTS])
        rank = sb("rank", [P, COLS, EXPERTS])
        cmp_t = sb("cmp_t", [P, EXPERTS, 16])
        tiles_e = sb("tiles_e", [P, EXPERTS])
        lt_t = sb("lt_t", [P, EXPERTS, EXPERTS])
        base_e = sb("base_e", [P, EXPERTS])
        end_e = sb("end_e", [P, EXPERTS])
        base_s = sb("base_s", [P, EXPERTS])
        slot_f = sb("slot_f", [P, COLS])
        slot_u = sb("slot_u", [P, COLS], U32)
        te_t = sb("te_t", [P, N_TILES, EXPERTS])
        te_f = sb("te_f", [P, N_TILES])
        te_i = sb("te_i", [P, N_TILES], I32)
        zero = sb("zero", [P, P])
        stats2 = sb("stats2", [P, TJ, 6])
        mv2 = sb("mv2", [P, TJ, 2])
        var_eps2 = sb("var_eps2", [P, TJ])
        rstd2 = sb("rstd2", [P, TJ])
        h1m_z2 = sb("h1m_z2", [P, 2, TJ, P])
        h1m, z2 = h1m_z2[:, 0], h1m_z2[:, 1]
        y_sb = sb("y_sb", [P, ROUND, P])
        sel_sb = h1m_z2[:].rearrange("p a j d -> p (a j d)")[:, 0:C_END - C_SEL]

        with nc.sbuf_tensor("w_r", [P, 2, WIDE_TAPS * P], F32R) as w_r, \
                nc.sbuf_tensor("x_r", [P, 2, CTX, GROUP], F32R) as x_r:
            pass
        w1_now = sb("w1_now", [P, ROUND, FFN])
        hidT = sb("hidT", [P, ROUND, FC, P])
        zs = sb("zs", [P, ROUND, P])
        zsT = sb("zsT", [P, ROUND, P])
        g_sb = sb("g_sb", [P, COLS, P])

        tok_ps = ctx.enter_context(nc.psum_tensor("tok_ps", [P, 2, 512], F32))
        s_ps = ctx.enter_context(nc.psum_tensor("s_ps", [P, 4, 512], F32))
        m_ps = ctx.enter_context(nc.psum_tensor("m_ps", [P, 2, 512], F32))

        z_dram = nc.dram_tensor("z_slots", (N_TILES * P, P), F32, kind="Internal").ap()
        y_dram = nc.dram_tensor("y_slots", (N_TILES * P, P), F32, kind="Internal").ap()

        ident = c_sb[:, C_IDENT:C_IDENT + P]
        wide_taps = wt_sb[:, 0:WIDE_TAPS].rearrange("p c d -> p (c d)")
        out_rows = out.rearrange("b n d -> (b n) d")

        consts_in, sel_in, small_in = sem("consts_in"), sem("sel_in"), sem("small_in")
        wqkv_in, agg_in = sem("wqkv_in"), sem("agg_in")
        idx_in, ew_in = sem("idx_in"), sem("ew_in")
        x_in0 = [sem(f"x_in0_{m}") for m in range(R4)]
        x_in = [sem(f"x_in{g}") for g in range(1, BATCH // GROUP)]
        wt_in = [sem(f"wt_in{s}") for s in range(len(WT_PARTS))]
        w1_in, w2_in = sem("w1_in"), sem("w2_in")
        zero_set, z_cleared = sem("zero_set"), sem("z_cleared")
        pads_set, psum_set = sem("pads_set"), sem("psum_set")
        consts_r = sem("consts_r")
        comb_ready = sem("comb_ready")
        w_hi_ready, w_lo_ready = sem("w_hi_ready"), sem("w_lo_ready")
        x_hi_ready, x_lo_ready = sem("x_hi_ready"), sem("x_lo_ready")
        tok_done, hT_ready = sem("tok_done"), sem("hT_ready")
        h_turned, h_ready = sem("h_turned"), sem("h_ready")
        stats_ready, mv_ready = sem("stats_ready"), sem("mv_ready")
        eps_added, rstd_ready, hb_ready = sem("eps_added"), sem("rstd_ready"), sem("hb_ready")
        z_ready, z_turned, zT_ready = sem("z_ready"), sem("z_turned"), sem("zT_ready")
        qk_done, v_done = sem("qk_done"), sem("v_done")
        hi_ready, lo_ready, v_ready = sem("hi_ready"), sem("lo_ready"), sem("v_ready")
        stacked, q_st_ready, k_st_ready = sem("stacked"), sem("q_st_ready"), sem("k_st_ready")
        s1_done, max_ready = sem("s1_done"), sem("max_ready")
        max_placed, q_shifted = sem("max_placed"), sem("q_shifted")
        s2_done, probs_ready = sem("s2_done"), sem("probs_ready")
        pv_done, o_raw_ready, o_turned = sem("pv_done"), sem("o_raw_ready"), sem("o_turned")
        rden_ready, o_ready, on_turned, oT_ready = (
            sem("rden_ready"), sem("o_ready"), sem("on_turned"), sem("oT_ready"))
        agg_done, h1_ready = sem("agg_done"), sem("h1_ready")
        stored, h1_free = sem("stored"), sem("h1_free")
        route = sem("route")
        onehot_ready, counted = sem("onehot_ready"), sem("counted")
        routed = sem("routed")
        h1m_in, stats2_ready, mv2_ready = sem("h1m_in"), sem("stats2_ready"), sem("mv2_ready")
        eps2_added, rstd2_ready, z2_ready = sem("eps2_added"), sem("rstd2_ready"), sem("z2_ready")
        scattered = sem("scattered")
        zs_in = [sem(f"zs_in{h}") for h in range(2)]
        zs_turned, zsT_ready = sem("zs_turned"), sem("zsT_ready")
        w1_ready, hid_done, hidT_ready = sem("w1_ready"), sem("hid_done"), sem("hidT_ready")
        y_done, y_ready = sem("y_done"), sem("y_ready")
        y_out = [sem(f"y_out{h}") for h in range(2)]
        gathered = [sem(f"gathered{i}") for i in range(COLS // 4)]
        combined = sem("combined")
        final_out = sem("final_out")

        block = ctx.enter_context(nc.Block())

        @block.sync
        def _(sp):
            def load_wt(n):
                lo, hi = WT_PARTS[n]
                sp.dma_start(wt_sb[:, lo:hi], wt[:, lo:hi]).then_inc(wt_in[n], 16)

            for m in range(R4):
                if m < 2:
                    load_wt(m)
                sp.dma_start(x_sb[:, 0:GROUP, m], x[:, 0:GROUP, m]).then_inc(x_in0[m], 16)
            for n in range(2, len(WT_PARTS)):
                load_wt(n)
            for g in range(1, BATCH // GROUP):
                gs = slice(GROUP * g, GROUP * (g + 1))
                sp.dma_start(x_sb[:, gs], x[:, gs]).then_inc(x_in[g - 1], 16)
            sp.dma_start(w1_sb[:], w1.rearrange("e h f -> h e f")).then_inc(w1_in, 16)
            sp.dma_start(w2_sb[:], w2.rearrange("e (c p) d -> p e c d", p=P)).then_inc(w2_in, 16)
            sp.wait_ge(zero_set, 1)
            sp.dma_start(z_dram.rearrange("(i p) d -> p i d", p=P),
                         zero[:].unsqueeze(1).to_broadcast([P, N_TILES, P])).then_inc(z_cleared, 16)

            def store_h1(b, par):
                to = out[b] if isinstance(b, int) else out[bass.ds(b, 1)].squeeze(0)
                sp.wait_ge(h1_ready, b + 1)
                sp.dma_start(to[0:N0, :], h1[:, par, 0, :]).then_inc(stored, 16)
                sp.dma_start(to[N0:N, :], h1[0:N1, par, 1, :]).then_inc(stored, 16)
                sp.wait_ge(stored, b * 32 + 32)
                sp.sem_inc(h1_free, 1)

            with sp.Fori(0, H1M_AFTER // 2) as i:
                for par in range(2):
                    store_h1(i * 2 + par, par)

            sp.wait_ge(stored, 32 * FFN_BATCHES)
            sp.dma_start(h1m, out_rows[0:T_FFN].rearrange("(j p) d -> p j d", p=P)).then_inc(h1m_in, 16)

            def rows(dram, tiles):
                return dram[tiles[0] * P:(tiles[-1] + 1) * P, :].rearrange("(i p) d -> p i d", p=P)

            def load_zs(n):
                for h in range(2):
                    tiles = part_tiles(n, h)
                    if n:
                        sp.wait_ge(zs_turned, 2 * n - 1 + h)
                    sp.dma_start(zs[:, h * PART:h * PART + len(tiles), :],
                                 rows(z_dram, tiles)).then_inc(zs_in[h], 16)

            def store_y(n):
                for h in range(2):
                    tiles = part_tiles(n, h)
                    sp.wait_ge(y_ready, 2 * n + h + 1)
                    sp.dma_start(rows(y_dram, tiles), y_sb[:, h * PART:h * PART + len(tiles), :]).then_inc(y_out[h], 16)

            for b in range(H1M_AFTER, EXPERT_SLOT):
                if b == EXPERT_SLOT - 1:
                    sp.wait_ge(scattered, 16 * COLS)
                    sp.wait_ge(tok_done, 3 * G_LAST + 2)
                    load_zs(0)
                store_h1(b, b % 2)
            for b in range(EXPERT_SLOT, EXPERT_SLOT + ROUNDS + 1):
                n = b - EXPERT_SLOT
                if n:
                    store_y(n - 1)
                if n + 1 < ROUNDS:
                    load_zs(n + 1)
                store_h1(b, b % 2)
            for b in range(EXPERT_SLOT + ROUNDS + 1, BATCH - 1):
                store_h1(b, b % 2)
            for lo, hi in FINAL_PARTS:
                sp.wait_ge(combined, TOP_K * hi)
                sp.dma_start(out_rows[lo * P:hi * P].rearrange("(j p) d -> p j d", p=P),
                             h1m[:, lo:hi]).then_inc(final_out, 16)
            store_h1(BATCH - 1, (BATCH - 1) % 2)
            sp.wait_ge(final_out, 16 * len(FINAL_PARTS))

        @block.gpsimd
        def _(pool):
            g = nc.gpsimd
            g.memset(zero[:], 0.0).then_inc(zero_set, 1)
            pool.sem_inc(h1_free, 2)
            g.memset(eps_t[:], EPS)
            g.memset(mhalf_t[:], -0.5)
            g.memset(qk_hi[:, :, N:NE].bitcast(F32), 0.0)
            g.memset(qk_lo[:, :, N:NE].bitcast(F32), 0.0)
            g.memset(nmax[:].bitcast(F32), 0.0)
            g.memset(v_aug[:], 0.0).then_inc(pads_set, 1)
            pool.wait_ge(pads_set, 1)
            g.memset(v_aug[:, :, :, :, DH:DH + 1], 1.0).then_inc(pads_set, 1)

            def stage1(b, par):
                pool.wait_ge(mv_ready, b * 2 + 2)
                g.tensor_tensor(var_eps[:], mv[:, :, 1], eps_t[:, 0:2], ALU.add).then_inc(eps_added, 1)
                pool.wait_ge(eps_added, b + 1)
                g.tensor_tensor(rstd[:], var_eps[:], mhalf_t[:, 0:2], ALU.pow).then_inc(rstd_ready, 1)
                pool.wait_ge(h_ready, b + 1)
                g.tensor_tensor(hb[:, par], h_sb[:], bagg_sb[:].unsqueeze(1).to_broadcast([P, 2, P]),
                                ALU.add).then_inc(hb_ready, 1)

            def x_of(group):
                return x_sb[:, bass.ds(group * GROUP, GROUP)].rearrange("p b r q -> p (r q) b")

            def split_hi(group):
                g.tensor_copy(x_r[:, 0], x_of(group)).then_inc(x_hi_ready, 1)

            def split_lo(group):
                pool.wait_ge(x_hi_ready, group)
                g.tensor_tensor(mark[:], eps_t[:, 0:1], eps_t[:, 0:1], ALU.add)
                g.tensor_tensor(x_r[:, 1], x_of(group), x_r[:, 0].bitcast(F32), ALU.subtract).then_inc(x_lo_ready, 1)

            pool.wait_ge(x_in[0], 16)
            split_hi(1)
            pool.wait_ge(agg_in, 32)
            stage1(0, 0)
            split_lo(1)
            for q in x_in[1:]:
                pool.wait_ge(q, 16)
            with pool.Fori(0, G_PREP) as i:
                for j in range(1, GROUP + 1):
                    if j == GROUP:
                        pool.wait_ge(tok_done, i * 3 + 5)
                        split_hi(i + 2)
                        split_lo(i + 2)
                    stage1(i * GROUP + j, j % 2)

            def scatter(c):
                pool.wait_ge(z2_ready, c // TOP_K + 1)
                g.indirect_dma_start(
                    z_dram, bass.IndirectOffsetOnAxis(ap=slot_u[:, c:c + 1], axis=0),
                    z2[:, c // TOP_K, :], None).then_inc(scattered, 16)

            def gather(c):
                g.indirect_dma_start(
                    g_sb[:, c, :], None, y_dram,
                    bass.IndirectOffsetOnAxis(ap=slot_u[:, c:c + 1], axis=0)).then_inc(gathered[c // 4], 16)

            def fetch_w1(n, h):
                for i in part_tiles(n, h):
                    e = pool.value_load(te_i[0:1, i:i + 1], min_val=0, max_val=EXPERTS - 1)
                    if n:
                        pool.wait_ge(hid_done, i - ROUND + 1)
                    g.tensor_copy(w1_now[:, i % ROUND, :],
                                  w1_sb[:, bass.ds(e, 1), :].rearrange("p a f -> p (a f)")).then_inc(w1_ready, 1)

            first = G_PREP * GROUP
            stage1(first + 1, 1)
            pool.wait_ge(mv2_ready, TJ)
            g.tensor_tensor(var_eps2[:], mv2[:, :, 1], eps_t[:], ALU.add).then_inc(eps2_added, 1)
            pool.wait_ge(eps2_added, 1)
            g.tensor_tensor(rstd2[:], var_eps2[:], mhalf_t[:], ALU.pow).then_inc(rstd2_ready, 1)
            pool.wait_ge(routed, 1)
            pool.wait_ge(z_cleared, 16)
            for c in range(COLS // 2):
                scatter(c)
            stage1(first + 2, 0)
            for c in range(COLS // 2, COLS):
                scatter(c)
            pool.wait_ge(w1_in, 16)
            pool.wait_ge(tok_done, 3 * G_LAST + 2)
            fetch_w1(0, 0)
            stage1(first + 3, 1)
            fetch_w1(0, 1)
            for n in range(1, ROUNDS):
                fetch_w1(n, 0)
                stage1(first + 3 + n, (first + 3 + n) % 2)
                fetch_w1(n, 1)
            for b in range(first + 3 + ROUNDS, BATCH):
                stage1(b, b % 2)
            for h in range(2):
                pool.wait_ge(y_out[h], 16 * ROUNDS)
            for c in range(COLS):
                gather(c)

        @block.scalar
        def _(act):
            s = nc.scalar

            def stage1_head(b, first=False):
                if not first:
                    act.wait_ge(hb_ready, b)
                act.wait_ge(h_turned, b + 1)
                s.copy(h_sb[:], m_ps[:, 0, 0:2 * P].rearrange("p (t d) -> p t d", t=2)).then_inc(h_ready, 1)

            def stage1_zT(b):
                act.wait_ge(z_turned, b + 1)
                s.copy(zT[:], m_ps[:, 1, 0:N]).then_inc(zT_ready, 1)

            def stage1_hi(b):
                act.wait_ge(qk_done, b + 1)
                s.copy(qk_hi[:, :, 0:N], m_ps[:, 0, 0:2 * N].rearrange("p (w n) -> p w n", w=2)).then_inc(hi_ready, 1)

            def stage1_v(b, par):
                act.wait_ge(v_done, b + 1)
                s.copy(v_aug[:, par, :, :, 0:DH],
                       m_ps[:, 1, 0:2 * P].rearrange("p (t h d) -> p t h d", t=2, h=HEADS)).then_inc(v_ready, 1)

            def stage1_q(b):
                for f in range(2):
                    act.wait_ge(stacked, b * 2 + (f + 1))
                    s.copy(q_st[:, 2 * f:2 * f + 2, :].rearrange("p j n -> p (j n)"),
                           s_ps[:, 2 * f, 0:2 * NE]).then_inc(q_st_ready, 1)

            def exps(b, t, f):
                n = TILE_N[t]
                act.wait_ge(s2_done, b * 4 + (2 * t + f + 1))
                s.activation(probs[0:n, t, f].rearrange("p r j n -> p r (j n)"),
                             s_ps[0:n, 2 * f:2 * f + 2, 0:2 * NE], ACT.Exp,
                             scale=DH ** -0.5).then_inc(probs_ready, 1)

            def stage2_oraw(b):
                act.wait_ge(pv_done, b + 1)
                s.copy(o_raw[:], m_ps[:, 0, 0:2 * N].rearrange("p (r n) -> p r n", r=2)).then_inc(o_raw_ready, 1)

            def stage2_oT(b):
                act.wait_ge(on_turned, b + 1)
                s.copy(o_T[:], m_ps[:, 0, 0:N]).then_inc(oT_ready, 1)

            def slot(b, par, n=None):
                stage1_head(b + 1)
                exps(b, 0, 0)
                stage1_zT(b + 1)
                exps(b, 0, 1)
                stage1_hi(b + 1)
                exps(b, 1, 0)
                exps(b, 1, 1)
                stage1_q(b + 1)
                stage1_v(b + 1, 1 - par)
                gelus(n, 0, 1)
                stage2_oraw(b)
                gelus(n, 1, 4)
                stage2_oT(b)
                gelus(n, 4, ROUND)

            def gelus(n, lo, hi):
                for i in tiles_of(n, lo, hi):
                    act.wait_ge(hid_done, i + 1)
                    s.activation(hidT[:, i % ROUND].rearrange("p c s -> p (c s)"), tok_ps[:, i % 2, :],
                                 ACT.Gelu).then_inc(hidT_ready, 1)

            act.dma_start(ei_sb[:], ei.rearrange("(j p) k -> p j k", p=P)).then_inc(idx_in, 16)
            act.dma_start(comb[:], pos).then_inc(small_in, 16)
            act.dma_start(bias_sb[:], bias).then_inc(small_in, 16)
            act.dma_start(c_sb[:], consts[:, 0:C_SEL]).then_inc(consts_in, 16)
            act.dma_start(wqkv_sb[:], wqkv).then_inc(wqkv_in, 16)
            act.dma_start(bagg_sb[:], bagg).then_inc(agg_in, 16)
            act.dma_start(wagg_sb[:], wagg).then_inc(agg_in, 16)
            act.dma_start(sel_sb, consts[:, C_SEL:C_END]).then_inc(sel_in, 16)
            act.dma_start(ew_sb[:], ew.rearrange("(j p) k -> p j k", p=P)).then_inc(ew_in, 16)
            act.wait_ge(consts_in, 16)
            s.activation(warm[:], c_sb[:, C_KONE:C_KONE + 1], ACT.Exp)
            for n in range(4):
                act.wait_ge(wt_in[n], 16)
            s.copy(w_r[:, 0], wide_taps).then_inc(w_hi_ready, 1)
            act.wait_ge(pads_set, 2)
            stage1_head(0, True)
            stage1_zT(0)
            stage1_hi(0)
            stage1_q(0)
            stage1_v(0, 0)
            with act.Fori(0, G_PREP) as g:
                for j in range(GROUP):
                    slot(g * GROUP + j, j % 2)
            for b in range(G_PREP * GROUP, BATCH - 1):
                slot(b, b % 2, b - EXPERT_SLOT)
            for t in range(2):
                for f in range(2):
                    exps(BATCH - 1, t, f)
            for r, src in enumerate((m_ps[:, 0, 0:N], tok_ps[:, 0, 0:N])):
                act.wait_ge(pv_done, BATCH + r)
                s.copy(o_raw[:, r, :], src).then_inc(o_raw_ready, 1)
            stage2_oT(BATCH - 1)

        @block.vector
        def _(dve):
            v = nc.vector
            v.memset(m_ps[:], 0.0).then_inc(psum_set, 1)
            dve.wait_ge(consts_in, 16)
            v.tensor_copy(ident_r[:], ident).then_inc(consts_r, 1)
            dve.wait_ge(small_in, 32)
            for i in range(3):
                v.tensor_scalar(comb[:, N_AT[i]:N_AT[i] + N_SCALE[i]], comb[:, N_AT[i]:N_AT[i] + N_SCALE[i]],
                                bias_sb[:, i:i + 1], bias_sb[:, 3 + i:4 + i], ALU.add, ALU.add).then_inc(comb_ready, 1)
            dve.wait_ge(comb_ready, 3)

            steps = [0]

            def link(ins):
                steps[0] += 1
                ins.then_inc(route, 1)
                dve.wait_ge(route, steps[0])

            dve.wait_ge(idx_in, 16)
            link(v.tensor_copy(ei_f[:], ei_sb[:].rearrange("p j k -> p (j k)")))
            v.tensor_tensor(onehot[:], ei_f[:].unsqueeze(2).to_broadcast([P, COLS, EXPERTS]),
                            c_sb[:, C_IOTA:C_IOTA + P].rearrange("p (c e) -> p c e", e=EXPERTS),
                            ALU.is_equal).then_inc(onehot_ready, 1)
            link(v.memset(before[:, 0, :], 0.0))
            dve.wait_ge(counted, 2)
            for c in range(COLS):
                link(v.tensor_tensor(before[:, c + 1, :], before[:, c, :],
                                     s_ps[:, 1, c * EXPERTS:(c + 1) * EXPERTS], ALU.add))
            total = before[:, COLS, :]
            link(v.tensor_tensor(cmp_t[:], total.unsqueeze(2).to_broadcast([P, EXPERTS, 16]),
                                 c_sb[:, C_THR:C_THR + P].rearrange("p (e m) -> p e m", m=16), ALU.is_gt))
            link(v.tensor_reduce(tiles_e[:], cmp_t[:], AX_X, ALU.add))
            link(v.tensor_tensor(lt_t[:], tiles_e[:].unsqueeze(1).to_broadcast([P, EXPERTS, EXPERTS]),
                                 c_sb[:, C_LT:C_LT + 64].rearrange("p (e f) -> p e f", f=EXPERTS), ALU.mult))
            link(v.tensor_reduce(base_e[:], lt_t[:], AX_X, ALU.add))
            link(v.tensor_tensor(end_e[:], base_e[:], tiles_e[:], ALU.add))
            link(v.tensor_scalar(base_s[:], base_e[:], float(P), None, ALU.mult))
            link(v.tensor_tensor(rank[:], before[:, 0:COLS, :],
                                 s_ps[:, 0, 0:P].rearrange("p (c e) -> p c e", e=EXPERTS), ALU.add))
            link(v.tensor_tensor(rank[:], rank[:], base_s[:].unsqueeze(1).to_broadcast([P, COLS, EXPERTS]), ALU.add))
            link(v.tensor_tensor(rank[:], rank[:], onehot[:], ALU.mult))
            link(v.tensor_reduce(slot_f[:], rank[:], AX_X, ALU.add))
            link(v.tensor_copy(slot_u[:], slot_f[:]))
            link(v.tensor_tensor(te_t[:], end_e[:].unsqueeze(1).to_broadcast([P, N_TILES, EXPERTS]),
                                 c_sb[:, C_TILE:C_TILE + N_TILES * EXPERTS].rearrange("p (i e) -> p i e", e=EXPERTS),
                                 ALU.is_le))
            link(v.tensor_reduce(te_f[:], te_t[:], AX_X, ALU.add))
            v.tensor_scalar(te_i[:], te_f[:], float(EXPERTS - 1), None, ALU.min).then_inc(routed, 1)

            def hT_evac(g):
                for i, src in enumerate((tok_ps[:, 0, 0:GROUP * N_SCALE[0]],
                                         tok_ps[:, 1, 0:GROUP * N_SCALE[1]],
                                         tok_ps[:, 1, GROUP * N_SCALE[1]:GROUP * (N_SCALE[1] + N_SCALE[2])])):
                    a, n = N_AT[i], N_SCALE[i]
                    if i < 2:
                        dve.wait_ge(tok_done, g * 3 + (1 if i == 0 else 3))
                    v.tensor_tensor(hT[:, :, a:a + n], src.rearrange("p (n b) -> p b n", b=GROUP),
                                    comb[:, a:a + n].unsqueeze(1).to_broadcast([P, GROUP, n]),
                                    ALU.add).then_inc(hT_ready, 1)

            def stage1_stats(b):
                dve.wait_ge(h_ready, b + 1)
                for t in range(2):
                    v.bn_stats(stats[:, t, :], h_sb[:, t, :]).then_inc(stats_ready, 1)
                dve.wait_ge(stats_ready, b * 2 + 2)
                v.tensor_copy(counts[:], stats[:, :, 0])
                for t in range(2):
                    v.bn_aggr(mv[:, t, :], stats[:, t, :]).then_inc(mv_ready, 1)

            def stage1_z(b):
                dve.wait_ge(rstd_ready, b + 1)
                for t in range(2):
                    v.tensor_scalar(z_sb[:, t, :], h_sb[:, t, :], mv[:, t, 0:1], rstd[:, t:t + 1],
                                    ALU.subtract, ALU.mult).then_inc(z_ready, 1)

            def stage1_lo(b):
                dve.wait_ge(hi_ready, b + 1)
                v.tensor_tensor(qk_lo[:, :, 0:N], m_ps[:, 0, 0:2 * N].rearrange("p (w n) -> p w n", w=2),
                                qk_hi[:, :, 0:N].bitcast(F32), ALU.subtract).then_inc(lo_ready, 1)

            def stage1_max(b, t):
                n = TILE_N[t]
                for f in range(2):
                    dve.wait_ge(s1_done, b * 4 + (2 * t + f + 1))
                    dst = nmax[0:n, t].rearrange("p (r m) -> p r m", r=2)[
                        :, :, MAX_ROW + 2 * f:MAX_ROW + 2 * f + 2]
                    src = s_ps[0:n, 2 * f:2 * f + 2, 0:2 * NE].rearrange("p r (j n) -> p r j n", j=2)[:, :, :, 0:N]
                    v.tensor_reduce(dst, src, AX_X, ALU.max, negate=True).then_inc(max_ready, 1)

            def stage1_k(b):
                for f in range(2):
                    dve.wait_ge(stacked, b * 2 + (f + 1))
                    v.tensor_tensor(k_st[:, 2 * f:2 * f + 2, :],
                                    s_ps[:, 2 * f + 1, 0:2 * NE].rearrange("p (j n) -> p j n", j=2),
                                    c_sb[:, C_KONE + 2 * f:C_KONE + 2 * f + 2].unsqueeze(2).to_broadcast([P, 2, NE]),
                                    ALU.add).then_inc(k_st_ready, 1)

            def stage2_shift(b):
                dve.wait_ge(max_placed, b + 1)
                for f in range(2):
                    qv = q_st[:, 2 * f:2 * f + 2, :]
                    v.tensor_tensor(qv, s_ps[:, 2, 0:NE].unsqueeze(1).to_broadcast([P, 2, NE]),
                                    qv.bitcast(F32), ALU.add).then_inc(q_shifted, 1)

            def stage2_norm(b):
                dve.wait_ge(o_turned, b + 1)
                for t in range(2):
                    n = TILE_N[t]
                    o = m_ps[0:n, 1, 256 * t:256 * (t + 1)].rearrange("p (h e) -> p h e", e=32)
                    v.reciprocal(rden[0:n, t, :], o[:, :, DH]).then_inc(rden_ready, 1)
                dve.wait_ge(rden_ready, b * 2 + 2)
                for t in range(2):
                    n = TILE_N[t]
                    o = m_ps[0:n, 1, 256 * t:256 * (t + 1)].rearrange("p (h e) -> p h e", e=32)
                    v.tensor_tensor(o_sb[0:n, t, :].rearrange("p (h d) -> p h d", d=DH), o[:, :, 0:DH],
                                    rden[0:n, t, :].unsqueeze(2).to_broadcast([n, HEADS, DH]),
                                    ALU.mult).then_inc(o_ready, 1)

            def stage2_h1(b, par):
                dve.wait_ge(agg_done, b + 1)
                dve.wait_ge(hb_ready, b + 1)
                dve.wait_ge(h1_free, b + 1)
                v.tensor_tensor(h1[:, par], m_ps[:, 1, 0:2 * P].rearrange("p (t d) -> p t d", t=2),
                                hb[:, par], ALU.add).then_inc(h1_ready, 1)

            def slot(b, par, j, g=None, n=-2, prepare=False):
                stage1_stats(b + 1)
                stage2_shift(b)
                stage1_z(b + 1)
                if prepare:
                    prepare_stats()
                if 0 < n <= ROUNDS:
                    y_evac(n - 1, 0)
                stage1_lo(b + 1)
                if prepare:
                    prepare_z()
                if 0 < n <= ROUNDS:
                    y_evac(n - 1, 1)
                if n == 0:
                    hT_evac(g + 1)
                if 0 <= n < ROUNDS:
                    zsT_evac(n, 0)
                stage1_k(b + 1)
                if 0 <= n < ROUNDS:
                    zsT_evac(n, 1)
                stage1_max(b + 1, 0)
                stage2_norm(b)
                stage1_max(b + 1, 1)
                if j == GROUP - 2 and g is not None and n != 0:
                    hT_evac(g + 1)
                stage2_h1(b, par)

            def prepare_stats():
                dve.wait_ge(h1m_in, 16)
                for i in range(TJ):
                    v.bn_stats(stats2[:, i, :], h1m[:, i, :]).then_inc(stats2_ready, 1)
                for i in range(TJ):
                    dve.wait_ge(stats2_ready, i + 1)
                    v.bn_aggr(mv2[:, i, :], stats2[:, i, :]).then_inc(mv2_ready, 1)

            def prepare_z():
                dve.wait_ge(rstd2_ready, 1)
                for i in range(TJ):
                    v.tensor_scalar(z2[:, i, :], h1m[:, i, :], mv2[:, i, 0:1], rstd2[:, i:i + 1],
                                    ALU.subtract, ALU.mult).then_inc(z2_ready, 1)

            def combine(cols):
                for c in cols:
                    i, k = c // TOP_K, c % TOP_K
                    dve.wait_ge(gathered[c // 4], 64)
                    dve.wait_ge(ew_in, 16)
                    if k:
                        dve.wait_ge(combined, c)
                    v.scalar_tensor_tensor(out=h1m[:, i, :], in0=g_sb[:, c, :], scalar=ew_sb[:, i, k:k + 1],
                                           in1=h1m[:, i, :], op0=ALU.mult, op1=ALU.add).then_inc(combined, 1)

            def zsT_evac(n, h):
                tiles = part_tiles(n, h)
                dve.wait_ge(zs_turned, 2 * n + h + 1)
                v.tensor_copy(zsT[:, h * PART:h * PART + len(tiles), :].rearrange("p i s -> p (i s)"),
                              tok_ps[:, h, 0:len(tiles) * P]).then_inc(zsT_ready, 1)

            def y_evac(n, h):
                tiles = part_tiles(n, h)
                dve.wait_ge(y_done, 2 * n + h + 1)
                if n:
                    dve.wait_ge(y_out[h], n * 16)
                v.tensor_copy(y_sb[:, h * PART:h * PART + len(tiles), :].rearrange("p i d -> p (i d)"),
                              tok_ps[:, h, 0:len(tiles) * P]).then_inc(y_ready, 1)

            hT_evac(0)
            stage1_stats(0)
            dve.wait_ge(sel_in, 16)
            v.tensor_copy(sel_r[:].rearrange("p a j m -> p (a j m)"),
                          sel_sb).then_inc(consts_r, 1)
            stage1_z(0)
            dve.wait_ge(w_hi_ready, 1)
            v.tensor_tensor(w_r[:, 1], wide_taps, w_r[:, 0].bitcast(F32), ALU.subtract).then_inc(w_lo_ready, 1)
            stage1_lo(0)
            stage1_k(0)
            stage1_max(0, 0)
            stage1_max(0, 1)
            with dve.Fori(0, G_PREP) as g:
                for j in range(GROUP):
                    slot(g * GROUP + j, j % 2, j, g)
            for b in range(G_PREP * GROUP, BATCH - 1):
                slot(b, b % 2, b % GROUP, G_PREP if b < G_LAST * GROUP else None, b - EXPERT_SLOT,
                     prepare=(b == G_PREP * GROUP))
            stage2_shift(BATCH - 1)
            combine(range(0, 3 * COLS // 4))
            stage2_norm(BATCH - 1)
            combine(range(3 * COLS // 4, COLS))
            stage2_h1(BATCH - 1, 1)

        @block.tensor
        def _(pe):
            def tok(g, taps, split=True):
                for c in taps:
                    i = 0 if c < TAP_AT[1] else 1 if c < TAP_AT[2] else 2
                    t = TAP_ORDER[i][c - TAP_AT[i]]
                    st = PATCHES[i] // 2 // R4
                    m, q0, n = t % R4, t // R4, N_SCALE[i]
                    q1 = q0 + (n - 1) * st + 1
                    o0 = 0 if i < 2 else GROUP * N_SCALE[1]
                    dst = tok_ps[:, min(i, 1), o0:o0 + GROUP * n].rearrange("p (n b) -> p n b", b=GROUP)
                    first, last = c == TAP_AT[i], c == TAP_AT[i] + PATCHES[i] - 1
                    if split and i < 2:
                        q = m * (CTX // R4)
                        for k, (w_part, x_part) in enumerate(((0, 0), (0, 1), (1, 0))):
                            mm = pe.matmul(dst, w_r[:, w_part, c * P:(c + 1) * P], x_r[:, x_part, q + q0:q + q1:st, :],
                                           start=first and k == 0, stop=last and k == 2)
                    else:
                        xs = x_sb[:, bass.ds(g * GROUP, GROUP), m, q0:q1:st].rearrange("p b q -> p q b")
                        mm = pe.matmul(dst, wt_sb[:, c, :], xs, start=first, stop=last)
                    if last:
                        mm.then_inc(tok_done, 1)

            def h_turn(j):
                pe.transpose(m_ps[:, 0, 0:P], hT[:, j, 0:N0], ident)
                pe.transpose(m_ps[0:N1, 0, P:2 * P], hT[:, j, N0:N], ident).then_inc(h_turned, 1)

            def z_turn(b):
                pe.wait_ge(z_ready, b * 2 + 2)
                pe.transpose(m_ps[:, 1, 0:N0], z_sb[:, 0, :], ident)
                pe.transpose(m_ps[:, 1, N0:N], z_sb[0:N1, 1, :], ident[0:N1, 0:N1]).then_inc(z_turned, 1)

            def project(b):
                pe.wait_ge(zT_ready, b + 1)
                for w in range(2):
                    mm = pe.matmul(m_ps[:, 0, w * N:(w + 1) * N], wqkv_sb[:, w * P:(w + 1) * P], zT[:],
                                   start=True, stop=True)
                mm.then_inc(qk_done, 1)
                pe.matmul(m_ps[:, 1, 0:P], zT[:, 0:N0], wqkv_sb[:, 2 * P:3 * P], start=True, stop=True)
                pe.matmul(m_ps[0:N1, 1, P:2 * P], zT[:, N0:N], wqkv_sb[:, 2 * P:3 * P],
                          start=True, stop=True).then_inc(v_done, 1)

            def stack(b, first=False):
                pe.wait_ge(lo_ready, b + 1)
                for f in range(2):
                    if not first:
                        pe.wait_ge(probs_ready, b * 4 + (f - 1))
                    for w in range(2):
                        for jj in range(2):
                            j = 2 * f + jj
                            dst = s_ps[:, 2 * f + w, jj * NE:(jj + 1) * NE]
                            pe.matmul(dst, sel_r[:, 2 * w, j, :], qk_hi[:, w, :], start=True, stop=False)
                            mm = pe.matmul(dst, sel_r[:, 2 * w + 1, j, :], qk_lo[:, w, :], start=False, stop=True)
                    mm.then_inc(stacked, 1)

            def scores(a, bb, t, f, done):
                n = TILE_N[t]
                for jj in range(2):
                    for r in range(2):
                        j = 2 * f + jj
                        mm = pe.matmul(s_ps[0:n, 2 * f + r, jj * NE:(jj + 1) * NE],
                                       a[64 * r:64 * r + 64, j, P * t:P * t + n], bb[64 * r:64 * r + 64, j, :],
                                       start=True, stop=True)
                mm.then_inc(done, 1)

            def s1(b, t, f):
                if t == 0:
                    pe.wait_ge(q_st_ready, b * 2 + (f + 1))
                    pe.wait_ge(k_st_ready, b * 2 + (f + 1))
                else:
                    pe.wait_ge(max_ready, b * 4 + (f + 1))
                scores(q_st, k_st, t, f, s1_done)

            def place_max(b):
                pe.wait_ge(max_ready, b * 4 + 4)
                for t in range(2):
                    n = TILE_N[t]
                    w = P if t == 0 else NE - P
                    mm = pe.matmul(s_ps[:, 2, P * t:P * t + w], nmax[0:n, t, :], ident_r[0:n, 0:w],
                                   start=True, stop=True)
                mm.then_inc(max_placed, 1)

            def s2(b, t, f):
                if t == 0:
                    pe.wait_ge(q_shifted, b * 2 + (f + 1))
                else:
                    pe.wait_ge(probs_ready, b * 4 + (f + 1))
                scores(k_st, q_st, t, f, s2_done)

            def pv(b, par, r, tiles=(0, 1), last=False):
                if r == 0:
                    pe.wait_ge(probs_ready, b * 4 + (2 * tiles[-1] + 2))
                    if not last:
                        pe.wait_ge(lo_ready, b + 2)
                bank = tok_ps[:, 0, 0:N] if last and r == 1 else m_ps[:, 0, r * N:(r + 1) * N]
                for t in tiles:
                    n = TILE_N[t]
                    for j in range(HALF):
                        mm = pe.matmul(bank[32 * j:32 * j + 32, :],
                                       v_aug[0:n, par, t, HALF * r + j, :],
                                       probs[0:n, t, j // 2, r, j % 2, 0:N],
                                       start=(t == 0), stop=(t == 1))
                if (r == 1 or last) and tiles[-1] == 1:
                    mm.then_inc(pv_done, 1)

            def o_turn(b, parts=1):
                pe.wait_ge(o_raw_ready, b + parts)
                for t in range(2):
                    n = TILE_N[t]
                    for r in range(2):
                        mm = pe.transpose(m_ps[0:n, 1, 256 * t + P * r:256 * t + P * (r + 1)],
                                          o_raw[:, r, P * t:P * t + n], ident)
                mm.then_inc(o_turned, 1)

            def on_turn(b):
                pe.wait_ge(o_ready, b * 2 + 2)
                pe.transpose(m_ps[:, 0, 0:N0], o_sb[:, 0, :], ident)
                pe.transpose(m_ps[:, 0, N0:N], o_sb[0:N1, 1, :], ident[0:N1, 0:N1]).then_inc(on_turned, 1)

            def aggregate(b):
                pe.wait_ge(oT_ready, b + 1)
                pe.matmul(m_ps[:, 1, 0:P], o_T[:, 0:N0], wagg_sb[:], start=True, stop=True)
                pe.matmul(m_ps[0:N1, 1, P:2 * P], o_T[:, N0:N], wagg_sb[:], start=True,
                          stop=True).then_inc(agg_done, 1)

            def weight(c):
                return 6 if c < TAP_AT[1] else 3 if c < TAP_AT[2] else 2

            SHARE = [[0, 8, 1, 9, 2, 10, 3, 11, 12], [4, 13, 5, 14, 6, 15, 7, 16, 17],
                     list(range(18, 35)), list(range(35, TAPS))]

            FILL = (0, 7, 0, 3, 0, 4, 1, 2, 3, 4)
            FILL_FIRST = (4, 7, 0, 3, 0, 6, 0, 0, 0, 0)

            for m in range(R4):
                if m < 2:
                    pe.wait_ge(wt_in[m], 16)
                pe.wait_ge(x_in0[m], 16)
                tok(0, range(2 * m, 2 * m + 2), split=False)
            for n, (lo, hi) in enumerate(WT_PARTS):
                if n < 2:
                    continue
                pe.wait_ge(wt_in[n], 16)
                tok(0, range(lo, hi), split=False)
                if n == 2:
                    pe.wait_ge(consts_in, 16)
                    pe.wait_ge(onehot_ready, 1)
                    oh = onehot[:].rearrange("p c e -> p (c e)")
                    for bank, c in enumerate((C_TRI, C_ONES)):
                        pe.matmul(s_ps[:, bank, 0:P], c_sb[:, c:c + P], oh, start=True,
                                  stop=True).then_inc(counted, 1)
            pe.wait_ge(psum_set, 1)
            pe.wait_ge(hT_ready, 3)
            h_turn(0)
            pe.wait_ge(x_in[0], 16)
            tok(1, SHARE[0][:-4], split=False)
            z_turn(0)
            tok(1, SHARE[0][-4:-2], split=False)
            pe.wait_ge(wqkv_in, 16)
            project(0)
            tok(1, SHARE[0][-2:], split=False)
            pe.wait_ge(agg_in, 32)
            pe.wait_ge(consts_r, 2)
            pe.wait_ge(routed, 1)
            stack(0, first=True)
            for t in range(2):
                for f in range(2):
                    s1(0, t, f)
            for q in x_in[1:]:
                pe.wait_ge(q, 16)
            pe.wait_ge(w_lo_ready, 1)
            pe.wait_ge(x_lo_ready, 1)

            def zs_turn(n, h):
                if not 0 <= n < ROUNDS:
                    return
                if n:
                    pe.wait_ge(y_ready, 2 * n - 1 + h)
                pe.wait_ge(zs_in[h], 16 * (n + 1))
                for k, i in enumerate(part_tiles(n, h)):
                    mm = pe.transpose(tok_ps[:, h, k * P:(k + 1) * P], zs[:, i % ROUND, :], ident)
                mm.then_inc(zs_turned, 1)

            def hidden(n, lo, hi):
                for i in tiles_of(n, lo, hi):
                    if i % ROUND < 2:
                        pe.wait_ge(zsT_ready, 2 * n + 2)
                    else:
                        pe.wait_ge(hidT_ready, i - 1)
                    pe.wait_ge(w1_ready, i + 1)
                    for c in range(FC):
                        mm = pe.matmul(tok_ps[:, i % 2, c * P:(c + 1) * P], w1_now[:, i % ROUND, c * P:(c + 1) * P],
                                       zsT[:, i % ROUND, :], start=True, stop=True)
                    mm.then_inc(hid_done, 1)

            def down(n, lo, hi):
                for i in tiles_of(n, lo, hi):
                    h, k = (i % ROUND) // PART, i % PART
                    e = pe.value_load(te_i[0:1, i:i + 1], min_val=0, max_val=EXPERTS - 1)
                    if k == 0:
                        pe.wait_ge(hidT_ready, min(n * ROUND + ROUND, N_TILES))
                    for c in range(FC):
                        mm = pe.matmul(tok_ps[:, h, k * P:(k + 1) * P], hidT[:, i % ROUND, c, :],
                                       w2_sb[:, bass.ds(e, 1), c, :].rearrange("p a d -> p (a d)"),
                                       start=(c == 0), stop=(c == FC - 1))
                    if i == part_tiles(n, h)[-1]:
                        mm.then_inc(y_done, 1)

            def slot(group, j, g=None, n=-2):
                b, par = group * GROUP + j, j % 2
                share = (j + 1) % GROUP
                left = list(SHARE[share]) if g is not None else []
                whole = sum(weight(c) for c in left)
                fills = FILL_FIRST if n == 0 else FILL

                def fill(k):
                    now = []
                    while left and whole - sum(weight(c) for c in left) < sum(fills[:k + 1]) * whole / sum(fills):
                        now.append(left.pop(0))
                    tok(g, now)

                if share == 0:
                    place_max(b)
                    pe.wait_ge(hT_ready, group * 3 + 6)
                h_turn(share)
                if g is not None and share == 0:
                    pe.wait_ge(x_lo_ready, group + 2)
                fill(0)
                if share:
                    place_max(b)
                down(n - 1, 0, 1)
                fill(1)
                down(n - 1, 1, 2)
                s2(b, 0, 0)
                s2(b, 0, 1)
                fill(2)
                down(n - 1, 2, 3)
                z_turn(b + 1)
                fill(3)
                down(n - 1, 3, 4)
                project(b + 1)
                s2(b, 1, 0)
                fill(4)
                down(n - 1, 4, 5)
                s2(b, 1, 1)
                fill(5)
                down(n - 1, 5, 6)
                if n == 0:
                    pe.wait_ge(hT_ready, 3 * (G_LAST + 1))
                    pe.wait_ge(w2_in, 16)
                zs_turn(n, 0)
                stack(b + 1)
                zs_turn(n, 1)
                pv(b, par, 0)
                s1(b + 1, 0, 0)
                hidden(n, 0, 1)
                pv(b, par, 1)
                s1(b + 1, 0, 1)
                fill(6)
                hidden(n, 1, 2)
                o_turn(b)
                fill(7)
                hidden(n, 2, 3)
                s1(b + 1, 1, 0)
                hidden(n, 3, 4)
                s1(b + 1, 1, 1)
                fill(8)
                on_turn(b)
                fill(9)
                hidden(n, 4, 5)
                aggregate(b)
                hidden(n, 5, 6)

            with pe.Fori(0, G_PREP) as g:
                for j in range(GROUP):
                    slot(g, j, g + (2 if j == GROUP - 1 else 1))
            for b in range(G_PREP * GROUP, BATCH - 1):
                slot(b // GROUP, b % GROUP, G_LAST if b < G_LAST * GROUP - 1 else None, b - EXPERT_SLOT)
            b = BATCH - 1
            place_max(b)
            for t in range(2):
                for f in range(2):
                    s2(b, t, f)
            for t in range(2):
                for r in range(2):
                    pv(b, 1, r, (t,), last=True)
            o_turn(b, 2)
            on_turn(b)
            aggregate(b)


def constants(np):
    c = np.zeros((P, C_END), np.float32)
    c[:, C_IDENT:C_IDENT + P] = np.eye(P)
    sel = np.zeros((P, 4, HALF, P), np.float32)
    for r in range(2):
        for j in range(HALF):
            for d in range(DH):
                src = (HALF * r + j) * DH + d
                row = 64 * r + d
                for which, blocks in enumerate(((0, 1), (2,), (0, 2), (1,))):
                    for blk in blocks:
                        sel[src, which, j, row + DH * blk] = 1.0
    c[:, C_SEL:C_SEL + 16 * P] = sel.reshape(P, -1)
    c[:, C_TRI:C_TRI + P] = np.triu(np.ones((P, P)), 1)
    c[:, C_ONES:C_ONES + P] = 1.0
    c[:, C_IOTA:C_IOTA + P] = np.tile(np.arange(EXPERTS), COLS)
    c[:, C_THR:C_THR + P] = np.tile(np.arange(16) * P, EXPERTS)
    c[:, C_LT:C_LT + 64] = np.tril(np.ones((EXPERTS, EXPERTS)), -1).reshape(-1)
    c[:, C_TILE:C_TILE + N_TILES * EXPERTS] = np.repeat(np.arange(N_TILES), EXPERTS)
    for j in range(HALF):
        c[MAX_ROW + j, C_KONE + j] = c[64 + MAX_ROW + j, C_KONE + j] = 1.0
    return c


def kernel(**inputs):
    import numpy as np
    import concourse.bacc as bacc
    from concourse.bass_utils import run_bass_kernel_spmd

    a = {k: np.asarray(v) for k, v in inputs.items()}
    arrays = {
        "x": a["x"].transpose(2, 0, 1).reshape(P, BATCH, CTX // R4, R4).transpose(0, 1, 3, 2),
        "wt": np.concatenate([a[f"L0_tok_W{i}"].reshape(P, p, P).transpose(2, 1, 0)[:, list(TAP_ORDER[i])]
                              for i, p in enumerate(PATCHES)], axis=1),
        "pos": np.concatenate([a[f"L0_tok_pos{i}"][0] for i in range(3)], axis=0).T,
        "bias": np.stack([a[f"L0_tok_b{i}"] for i in range(3)]
                         + [a["L0_tok_scale_emb"][i] for i in range(3)], axis=1),
        "wqkv": a["L0_attn_w_qkv"].T,
        "wagg": a["L0_attn_w_agg"].T,
        "bagg": np.broadcast_to(a["L0_attn_b_agg"][None, :], (P, P)),
        "consts": constants(np),
        "ew": a["L0_ffn_expert_weights"],
        "ei": a["L0_ffn_expert_indices"],
        "w1": a["L0_ffn_w1"],
        "w2": a["L0_ffn_w2"],
    }
    arrays = {k: np.ascontiguousarray(v) for k, v in arrays.items()}
    nc = bacc.Bacc("TRN2", target_bir_lowering=False, num_devices=1)
    aps = [nc.dram_tensor(k, v.shape, mybir.dt.from_np(v.dtype), kind="ExternalInput").ap() for k, v in arrays.items()]
    out = nc.dram_tensor("out", (BATCH, N, P), F32, kind="ExternalOutput").ap()
    build(nc, *aps, out)
    r = run_bass_kernel_spmd(nc, [arrays], core_ids=[0])
    return r.results[0]["out"]
```
